# Optimizing a Trainium2 kernel written in Bass

```python
import numpy as np
import jax
import jax.numpy as jnp

def _softmax(x, axis=-1):
    return jax.nn.softmax(x, axis=axis)

def _gelu(x):
    return jax.nn.gelu(x, approximate=True)

def _silu(x):
    return jax.nn.silu(x)

def _sigmoid(x):
    return jax.nn.sigmoid(x)

def _layernorm(x, axis=-1, eps=1e-05):
    m = jnp.mean(x, axis=axis, keepdims=True)
    v = jnp.var(x, axis=axis, keepdims=True)
    return (x - m) / jnp.sqrt(v + eps)

def _scatter_add(tgt, idx, src, axis=0):
    return tgt.at[idx].add(src)

def _segment_sum(src, seg, n):
    return jax.ops.segment_sum(src, seg, n)
kernel_name = 'mk_audio_tower_d1_tok_aud1d1024_r4_da87fd'

def setup_inputs(seed: int=0):
    np.random.seed(seed)
    _w = jnp.asarray

    def _rec_inputs():
        import jax
        import jax.numpy as jnp
        _rk = jax.random.key(seed)
        x = -9.80646e-05 + 1.00041 * jax.random.normal(jax.random.fold_in(_rk, 1), (32, 1024), jnp.float32)
        return x
    x = _rec_inputs()

    def _L0_tok_setup():
        import jax, jax.numpy as jnp
        import numpy as np
        P = 16
        key = jax.random.key(seed)
        ks = jax.random.split(key, 7)
        B, L = (128, 1024)
        I, H = (512, 256)
        F = 2 * P
        s_in = 1.0 / np.sqrt(F)
        s_mid = 1.0 / np.sqrt(I)
        return {'x': jax.random.normal(ks[0], (B, L), jnp.float32), 'W_h': jax.random.normal(ks[1], (I, F), jnp.float32) * s_in, 'b_h': jax.random.normal(ks[2], (I,), jnp.float32) * s_in, 'W_o': jax.random.normal(ks[3], (H, I), jnp.float32) * s_mid, 'b_o': jax.random.normal(ks[4], (H,), jnp.float32) * s_mid, 'W_r': jax.random.normal(ks[5], (H, F), jnp.float32) * s_in, 'b_r': jax.random.normal(ks[6], (H,), jnp.float32) * s_in}
    _L0_tok_all = _L0_tok_setup()
    _L0_tok_in = {k: v for k, v in _L0_tok_all.items() if k in ('W_h', 'b_h', 'W_o', 'b_o', 'W_r', 'b_r')}
    del _L0_tok_all

    def _L0_attn_setup():
        import jax, jax.numpy as jnp
        import numpy as np
        import math
        B, S, E, H = (2, 512, 256, 16)
        D = E // H
        key = jax.random.key(seed)
        ks = jax.random.split(key, 5)
        scale_p = 1.0 / math.sqrt(D)
        return {'x': jax.random.normal(ks[0], (B, S, E), dtype=jnp.float32), 'Wq': jax.random.normal(ks[1], (D, D), dtype=jnp.float32) * scale_p, 'Wk': jax.random.normal(ks[2], (D, D), dtype=jnp.float32) * scale_p, 'Wv': jax.random.normal(ks[3], (D, D), dtype=jnp.float32) * scale_p, 'W_out': jax.random.normal(ks[4], (E, E), dtype=jnp.float32) * (1.0 / math.sqrt(E)), 'b_out': jnp.zeros((E,), dtype=jnp.float32)}
    _L0_attn_all = _L0_attn_setup()
    _L0_attn_in = {k: v for k, v in _L0_attn_all.items() if k in ('Wq', 'Wk', 'Wv', 'W_out', 'b_out')}
    del _L0_attn_all

    def _L0_ffn_setup():
        import jax, jax.numpy as jnp
        import numpy as np
        B, N, D = (4, 512, 256)
        SPARSITY = 0.01
        key = jax.random.key(seed)
        k1, k2, k3 = jax.random.split(key, 3)
        x = jax.random.normal(k1, (B, N, D), dtype=jnp.float32)
        spatial = jax.random.normal(k2, (D, D), dtype=jnp.float32) * 0.02
        freq = jnp.fft.fft(spatial, axis=-1)
        k = int(D * SPARSITY)
        mag = jnp.abs(freq)
        kth = jax.lax.top_k(mag, k)[0][:, -1:]
        w_sparse = jnp.where(mag >= kth, freq, 0.0 + 0j)
        bias = jax.random.normal(k3, (D,), dtype=jnp.float32) * 0.01
        return {'x': x, 'w_freq_real': jnp.real(w_sparse).astype(jnp.float32), 'w_freq_imag': jnp.imag(w_sparse).astype(jnp.float32), 'bias': bias}
    _L0_ffn_all = _L0_ffn_setup()
    _L0_ffn_in = {k: v for k, v in _L0_ffn_all.items() if k in ('w_freq_real', 'w_freq_imag', 'bias')}
    del _L0_ffn_all
    return {'x': x, 'L0_tok_W_h': _L0_tok_in['W_h'], 'L0_tok_b_h': _L0_tok_in['b_h'], 'L0_tok_W_o': _L0_tok_in['W_o'], 'L0_tok_b_o': _L0_tok_in['b_o'], 'L0_tok_W_r': _L0_tok_in['W_r'], 'L0_tok_b_r': _L0_tok_in['b_r'], 'L0_attn_Wq': _L0_attn_in['Wq'], 'L0_attn_Wk': _L0_attn_in['Wk'], 'L0_attn_Wv': _L0_attn_in['Wv'], 'L0_attn_W_out': _L0_attn_in['W_out'], 'L0_attn_b_out': _L0_attn_in['b_out'], 'L0_ffn_w_freq_real': _L0_ffn_in['w_freq_real'], 'L0_ffn_w_freq_imag': _L0_ffn_in['w_freq_imag'], 'L0_ffn_bias': _L0_ffn_in['bias']}

def reference(x, L0_tok_W_h, L0_tok_b_h, L0_tok_W_o, L0_tok_b_o, L0_tok_W_r, L0_tok_b_r, L0_attn_Wq, L0_attn_Wk, L0_attn_Wv, L0_attn_W_out, L0_attn_b_out, L0_ffn_w_freq_real, L0_ffn_w_freq_imag, L0_ffn_bias):
    import jax
    import jax.numpy as jnp

    def _L0_tok_ref(x, W_h, b_h, W_o, b_o, W_r, b_r):
        import jax, jax.numpy as jnp
        import numpy as np
        P = 16
        B, L = x.shape
        pad = -L % P
        mask = jnp.ones_like(x)
        if pad > 0:
            x = jnp.pad(x, ((0, 0), (pad, 0)))
            mask = jnp.pad(mask, ((0, 0), (pad, 0)))
        xp = x.reshape(B, -1, P)
        mp = mask.reshape(B, -1, P)
        x_cat = jnp.concatenate([xp, mp], axis=-1)
        hid = jax.nn.silu(jnp.einsum('bnf,if->bni', x_cat, W_h) + b_h)
        out = jnp.einsum('bni,hi->bnh', hid, W_o) + b_o
        res = jnp.einsum('bnf,hf->bnh', x_cat, W_r) + b_r
        return out + res

    def _L0_attn_ref(x, Wq, Wk, Wv, W_out, b_out):
        import jax, jax.numpy as jnp
        import numpy as np
        import math
        B, S, E, H = (2, 512, 256, 16)
        D = E // H
        b, s, e = x.shape
        xh = x.reshape(b, s, H, D)
        q = jnp.einsum('bshd,ed->bshe', xh, Wq)
        k = jnp.einsum('bshd,ed->bshe', xh, Wk)
        v = jnp.einsum('bshd,ed->bshe', xh, Wv)
        energy = jnp.einsum('bqhd,bkhd->bhqk', q, k) / jnp.sqrt(jnp.float32(e))
        attn = jax.nn.softmax(energy, axis=-1)
        out = jnp.einsum('bhqk,bkhd->bqhd', attn, v).reshape(b, s, e)
        return out @ W_out.T + b_out

    def _L0_ffn_ref(x, w_freq_real, w_freq_imag, bias):
        import jax, jax.numpy as jnp
        import numpy as np
        B, N, D = (4, 512, 256)
        SPARSITY = 0.01
        w = jax.lax.complex(w_freq_real, w_freq_imag)
        x_freq = jnp.fft.fft(x, axis=-1)
        y_freq = jnp.einsum('bnd,do->bno', x_freq, w)
        y = jnp.real(jnp.fft.ifft(y_freq, axis=-1))
        return y + bias
    h = _L0_tok_ref(x, L0_tok_W_h, L0_tok_b_h, L0_tok_W_o, L0_tok_b_o, L0_tok_W_r, L0_tok_b_r)
    h = h + _L0_attn_ref(_layernorm(h, axis=-1), L0_attn_Wq, L0_attn_Wk, L0_attn_Wv, L0_attn_W_out, L0_attn_b_out)
    h = h + _L0_ffn_ref(_layernorm(h, axis=-1), L0_ffn_w_freq_real, L0_ffn_w_freq_imag, L0_ffn_bias)
    return h

_drawn_inputs = setup_inputs


def setup_inputs(seed=0):
    import zlib

    import numpy as np

    out = dict(_drawn_inputs(seed))
    spreads = {'L0_attn_b_out': (0.0, 0.1)}
    factors = {'L0_ffn_bias': 8.0}
    for name, (base, spread) in spreads.items():
        noise = np.random.default_rng([zlib.crc32(name.encode()), seed]).standard_normal(out[name].shape)
        drawn = base * np.exp(spread * noise) if base else spread * noise
        out[name] = jnp.asarray(drawn.astype(out[name].dtype))
    for name, factor in factors.items():
        out[name] = (out[name] * factor).astype(out[name].dtype)
    return out
```

```python
from contextlib import ExitStack

import concourse.bass as bass
import numpy as np
from concourse import mybir

F32 = mybir.dt.float32
ALU = mybir.AluOpType
ACT = mybir.ActivationFunctionType
AX_X = mybir.AxisListType.X

P = 128
BATCH, LENGTH = 32, 1024
PATCH = 16
TOK = LENGTH // PATCH
F = 2 * PATCH
HID = 512
NC = HID // P
D = 256
HEADS, HD = 16, 16
T = BATCH * TOK // P
GROUP = P // F
G = T // GROUP
HALF = D // P
QUADS = 4
EPS = 1e-5


def launch_constants():
    k = np.arange(P)[:, None].astype(np.float64)
    n = np.arange(D)[None, :].astype(np.float64)
    cosine = np.cos(2 * np.pi * k * n / D)
    sine = np.sin(2 * np.pi * k * n / D)
    sine[0] = np.cos(np.pi * n[0])
    r = np.arange(P)
    head_blocks = (r[:, None] // HD == r[None, :] // HD).astype(np.float32)
    head_sum = (r[:, None] // TOK == (np.arange(2 * HD)[None, :] // HD)).astype(np.float32)
    return {
        "identity": np.eye(P, dtype=np.float32),
        "head_blocks": head_blocks,
        "head_sum": head_sum,
        "cosine": cosine.astype(np.float32),
        "sine": sine.astype(np.float32),
    }


FOLDED = np.concatenate([np.arange(P), [P], np.arange(D - 1, P, -1)])


def audio_tower_kernel(nc, a, out):
    with ExitStack() as ctx:
        def sb(name, shape):
            return ctx.enter_context(nc.sbuf_tensor(name, shape, F32))

        def sem(name):
            return ctx.enter_context(nc.semaphore(name))

        ident = sb("ident", [P, P])
        blocks = sb("blocks", [P, P])
        head_sum = sb("head_sum_sb", [P, 2 * HD])
        cosine = sb("cosine_sb", [P, D])
        sine = sb("sine_sb", [P, D])
        wh_raw = sb("wh_raw", [P, NC, F])
        wh_rep = sb("wh_rep", [P, NC, GROUP, F])
        bh = sb("bh", [P, NC])
        wr_raw = sb("wr_raw", [P, HALF, F])
        wr_rep = sb("wr_rep", [P, HALF, GROUP, F])
        br = sb("br", [P, HALF])
        bo = sb("bo", [P, HALF])
        wo_raw = sb("wo_raw", [P, HALF, HID])
        wout_raw = sb("wout_raw", [P, HALF, D])
        whT = sb("whT", [P, HID])
        wrT = sb("wrT", [P, D])
        woT = sb("woT", [P, NC, D])
        woutT = sb("woutT", [P, HALF, D])
        wqk = sb("wqk", [HD, 3, HD])
        wrep = sb("wrep", [HD, 3, P])
        erep = sb("erep", [HD, P])
        score_w = sb("score_w", [P, P])
        wv_blocks = sb("wv_blocks", [P, P])
        value_w = sb("value_w", [P, HALF, D])
        fr = sb("fr", [P, 2, D])
        fi = sb("fi", [P, 2, D])
        rows = sb("rows", [P, 4, D])
        cols = sb("cols", [P, 4, P])
        halfway = sb("halfway", [P, 2, D])
        mix_w = sb("mix_w", [P, HALF, D])
        bout_bc = sb("bout_bc", [P, D])
        fbias_bc = sb("fbias_bc", [P, D])
        xcat = sb("xcat", [P, T, F])
        xcatT = sb("xcatT", [P, G, P])
        xg_hid = sb("xg_hid", [P, P])
        xg_res = sb("xg_res", [P, P])
        hidT = sb("hidT", [P, 2, HID])
        h_all = sb("h_all", [P, T, D])
        hb_all = sb("hb_all", [P, T, D])
        stats1 = sb("stats1", [P, T, 6])
        mv1 = sb("mv1", [P, T, 2])
        ve1 = sb("ve1", [P, T])
        rstd1 = sb("rstd1", [P, T])
        half_neg = sb("half_neg", [P, T])
        xblk = [sb(f"xblk{i}", [P, 2, D]) for i in range(2)]
        xzT = sb("xzT", [P, HALF, 2, P])
        xT = sb("xT", [P, HALF, P])
        qT = sb("qT", [P, HALF, P])
        rowmax = sb("rowmax", [P, QUADS, 4])
        probs = sb("probs", [P, QUADS, D])
        pT = sb("pT", [P, 2 * QUADS, P])
        inv_sum = sb("inv_sum", [P, D])
        onT = sb("onT", [P, HALF, P])
        h2 = sb("h2", [P, D])
        h2b = [sb(f"h2b{i}", [P, D]) for i in range(2)]
        stats2 = sb("stats2", [P, 6])
        mv2 = sb("mv2", [P, 2])
        ve2 = sb("ve2", [P, 1])
        rstd2 = sb("rstd2", [P, 1])
        xh2 = sb("xh2", [P, D])
        xh2T = sb("xh2T", [P, HALF, P])
        y = [sb(f"y{i}", [P, D]) for i in range(2)]

        bank = [ctx.enter_context(nc.psum_tensor(f"bank{i}", [P, 512], F32)) for i in range(8)]

        x_loaded, wh_loaded, wr_loaded, wo_loaded = sem("x_loaded"), sem("wh_loaded"), sem("wr_loaded"), sem("wo_loaded")
        ident_loaded, att_loaded, freq_loaded, bias_loaded = (
            sem("ident_loaded"), sem("att_loaded"), sem("freq_loaded"), sem("bias_loaded"))
        ones_set, zeros_set, rep_done = sem("ones_set"), sem("zeros_set"), sem("rep_done")
        rep_biased, bias_joined = sem("rep_biased"), sem("bias_joined")
        prep_pe, prep_copied = sem("prep_pe"), sem("prep_copied")
        folds, fold_step = sem("folds"), sem("fold_step")
        xg_hid_set, xg_res_set = sem("xg_hid_set"), sem("xg_res_set")
        hid_done, silu_done, mix_done = sem("hid_done"), sem("silu_done"), sem("mix_done")
        h_copied, hb_done, stats1_done, mv1_done, ve1_done, rstd1_done = (
            sem("h_copied"), sem("hb_done"), sem("stats1_done"), sem("mv1_done"), sem("ve1_done"), sem("rstd1_done"))
        xblk_set, xz_turned, xz_copied, x_added = sem("xblk_set"), sem("xz_turned"), sem("xz_copied"), sem("x_added")
        q_done, q_copied = sem("q_done"), sem("q_copied")
        scores_done, max_done, shifted, exp_done = sem("scores_done"), sem("max_done"), sem("shifted"), sem("exp_done")
        p_turned, p_copied, pv_done, inv_done, on_set = (
            sem("p_turned"), sem("p_copied"), sem("pv_done"), sem("inv_done"), sem("on_set"))
        proj_done, h2_done = sem("proj_done"), sem("h2_done")
        stats2_done, mv2_done, ve2_done, rstd2_done = sem("stats2_done"), sem("mv2_done"), sem("ve2_done"), sem("rstd2_done")
        h2b_done, xh2_set, xh2_turned, xh2_copied = sem("h2b_done"), sem("xh2_set"), sem("xh2_turned"), sem("xh2_copied")
        freq_done, y_set = sem("freq_done"), sem("y_set")
        y_stored = [sem("y_stored0"), sem("y_stored1")]

        x_tok = a["x"].rearrange("b (n f) -> (b n) f", f=PATCH).rearrange("(t p) f -> p t f", p=P)
        out_tok = out.rearrange("b n d -> (b n) d").rearrange("(t p) d -> p t d", p=P)

        def at_least(eng, s, n):
            if not (isinstance(n, int) and n <= 0):
                eng.wait_ge(s, n)

        block = ctx.enter_context(nc.Block())

        @block.sync
        def _(sp):
            for g in range(G):
                sp.dma_start(xcat[:, g * GROUP:(g + 1) * GROUP, 0:PATCH],
                             x_tok[:, g * GROUP:(g + 1) * GROUP, :]).then_inc(x_loaded, 16)
            sp.dma_start(wo_raw[:], a["W_o"].rearrange("(c p) i -> p c i", p=P)).then_inc(wo_loaded, 16)
            for name, dst in (("wr", fr), ("wi", fi)):
                sp.dma_start(dst[:], a[name].rearrange("(c p) n -> p c n", p=P)).then_inc(freq_loaded, 16)
            sp.dma_start(cosine[:], a["cosine"]).then_inc(freq_loaded, 16)
            sp.dma_start(sine[:], a["sine"]).then_inc(freq_loaded, 16)

            def store(t, par):
                sp.wait_ge(y_set, t + 1)
                sp.dma_start(out_tok[:, bass.ds(t, 1), :].rearrange("p o d -> p (o d)"),
                             y[par][:]).then_inc(y_stored[par], 16)

            with sp.Fori(0, T // 2) as u:
                store(2 * u, 0)
                store(2 * u + 1, 1)
            for par in range(2):
                sp.wait_ge(y_stored[par], 16 * (T // 2))

        @block.scalar
        def _(act):
            act.dma_start(ident[:], a["identity"]).then_inc(ident_loaded, 16)
            act.dma_start(wh_raw[:], a["W_h"].rearrange("(p c) f -> p c f", p=P)).then_inc(wh_loaded, 16)
            act.dma_start(bh[:], a["b_h"].rearrange("(p c) -> p c", p=P)).then_inc(wh_loaded, 16)
            act.dma_start(wr_raw[:], a["W_r"].rearrange("(p c) f -> p c f", p=P)).then_inc(wr_loaded, 16)
            act.dma_start(br[:], a["b_r"].rearrange("(p c) -> p c", p=P)).then_inc(wr_loaded, 16)
            act.dma_start(bo[:], a["b_o"].rearrange("(p c) -> p c", p=P)).then_inc(wr_loaded, 16)
            act.dma_start(bout_bc[:], a["b_out"].partition_broadcast(P)).then_inc(bias_loaded, 16)
            act.dma_start(fbias_bc[:], a["bias"].partition_broadcast(P)).then_inc(bias_loaded, 16)
            act.dma_start(wout_raw[:], a["W_out"].rearrange("(c p) i -> p c i", p=P)).then_inc(att_loaded, 16)
            for i, name in enumerate(("Wq", "Wk", "Wv")):
                act.dma_start(wqk[:, i, :], a[name]).then_inc(att_loaded, 16)
            act.dma_start(blocks[:], a["head_blocks"]).then_inc(att_loaded, 16)
            act.dma_start(head_sum[:], a["head_sum"]).then_inc(att_loaded, 16)

            def silu(t, par):
                act.wait_ge(hid_done, t + 1)
                if not (isinstance(t, int) and t < 2):
                    act.wait_ge(mix_done, t - 1)
                nc.scalar.activation(hidT[:, par, :], bank[par][:], ACT.Silu).then_inc(silu_done, 1)

            def copy_h(t, par):
                act.wait_ge(mix_done, t + 1)
                nc.scalar.activation(h_all[:, bass.ds(t, 1), :].rearrange("p o d -> p (o d)"),
                                     bank[2 + par][:, 0:D], ACT.Copy).then_inc(h_copied, 1)

            silu(0, 0)
            silu(1, 1)
            copy_h(0, 0)
            silu(2, 0)
            copy_h(1, 1)
            with act.Fori(1, T // 2 - 1) as u:
                silu(2 * u + 1, 1)
                copy_h(2 * u, 0)
                silu(2 * u + 2, 0)
                copy_h(2 * u + 1, 1)
            silu(T - 1, 1)
            copy_h(T - 2, 0)
            copy_h(T - 1, 1)

            def exponents(t):
                for j in range(QUADS):
                    act.wait_ge(shifted, QUADS * t + j + 1)
                    nc.scalar.activation(probs[:, j, :], probs[:, j, :], ACT.Exp).then_inc(exp_done, 1)

            def copy_xh2T(t):
                act.wait_ge(xh2_turned, t + 1)
                nc.scalar.activation(xh2T[:].rearrange("p a t -> p (a t)"), bank[5][:, 0:D],
                                     ACT.Copy).then_inc(xh2_copied, 1)

            def copy_xz(t):
                act.wait_ge(xz_turned, t + 1)
                nc.scalar.activation(xzT[:].rearrange("p a b t -> p (a b t)"), bank[4][:],
                                     ACT.Copy).then_inc(xz_copied, 1)

            def copy_p(t, half):
                act.wait_ge(p_turned, 2 * t + half + 1)
                nc.scalar.activation(pT[:, 4 * half:4 * half + 4, :].rearrange("p a t -> p (a t)"),
                                     bank[5 + half][:], ACT.Copy).then_inc(p_copied, 1)

            def copy_q(t):
                act.wait_ge(q_done, t + 1)
                nc.scalar.activation(qT[:].rearrange("p a t -> p (a t)"), bank[4][:, 0:D],
                                     ACT.Copy).then_inc(q_copied, 1)

            def step(i):
                late = not isinstance(i, int)
                if late or 0 <= i + 1 < T:
                    exponents(i + 1)
                if late or 0 <= i - 1:
                    copy_xh2T(i - 1)
                if late or i + 2 < T:
                    copy_xz(i + 2)
                if late or 0 <= i + 1 < T:
                    copy_p(i + 1, 0)
                if late or i + 2 < T:
                    copy_q(i + 2)
                if late or 0 <= i + 1 < T:
                    copy_p(i + 1, 1)

            for i in range(-2, 2):
                step(i)
            with act.Fori(1, T // 2 - 1) as u:
                step(2 * u)
                step(2 * u + 1)
            for i in range(T - 2, T + 1):
                step(i)

        @block.gpsimd
        def _(pool):
            nc.gpsimd.memset(xcat[:, :, PATCH:F], 1.0).then_inc(ones_set, 1)
            nc.gpsimd.memset(half_neg[:], -0.5).then_inc(ones_set, 1)
            for i in range(2):
                nc.gpsimd.memset(xblk[i][:], 0.0).then_inc(zeros_set, 1)

            pool.wait_ge(bias_loaded, 32)
            for g in range(G):
                tiles = slice(GROUP * g, GROUP * (g + 1))
                pool.wait_ge(h_copied, GROUP * (g + 1))
                nc.gpsimd.tensor_tensor(hb_all[:, tiles, :], h_all[:, tiles, :],
                                        bout_bc[:].unsqueeze(1).to_broadcast([P, GROUP, D]),
                                        ALU.add).then_inc(hb_done, 1)

            pool.wait_ge(freq_loaded, 64)
            u1, v1, u2, v2 = (rows[:, i, :] for i in range(4))
            nc.gpsimd.tensor_tensor(u1, fr[:, 0, :], fr[:, 1, :], ALU.add).then_inc(fold_step, 1)
            nc.gpsimd.tensor_tensor(v1, fi[:, 0, :], fi[:, 1, :], ALU.subtract).then_inc(fold_step, 1)
            nc.gpsimd.tensor_tensor(u2, fi[:, 0, :], fi[:, 1, :], ALU.add).then_inc(fold_step, 1)
            nc.gpsimd.tensor_tensor(v2, fr[:, 1, :], fr[:, 0, :], ALU.subtract).then_inc(fold_step, 1)
            pool.wait_ge(fold_step, 4)
            nc.gpsimd.tensor_copy(rows[0:1, 0, :], fr[0:1, 0, :]).then_inc(fold_step, 1)
            nc.gpsimd.tensor_copy(rows[0:1, 1, :], fr[0:1, 1, :]).then_inc(fold_step, 1)
            nc.gpsimd.tensor_copy(rows[0:1, 2, :], fi[0:1, 0, :]).then_inc(fold_step, 1)
            nc.gpsimd.tensor_copy(rows[0:1, 3, :], fi[0:1, 1, :]).then_inc(fold_step, 1)
            pool.wait_ge(fold_step, 8)
            for i in range(2):
                nc.gpsimd.tensor_tensor(cols[:, i, 1:P], rows[:, i, 1:P], rows[:, i, P + 1:D], ALU.add)
                nc.gpsimd.tensor_copy(cols[:, i, 0:1], rows[:, i, 0:1]).then_inc(folds, 1)
            for i in range(2):
                nc.gpsimd.tensor_tensor(cols[:, 2 + i, 1:P], rows[:, 2 + i, P + 1:D], rows[:, 2 + i, 1:P],
                                        ALU.subtract)
                nc.gpsimd.tensor_copy(cols[:, 2 + i, 0:1], rows[:, i, P:P + 1]).then_inc(folds, 1)

            pool.wait_ge(ve1_done, 1)
            nc.gpsimd.tensor_tensor(rstd1[:], ve1[:], half_neg[:], ALU.pow).then_inc(rstd1_done, 1)

            def inv_std(t):
                pool.wait_ge(ve2_done, t + 1)
                if not (isinstance(t, int) and t < 1):
                    pool.wait_ge(xh2_set, t)
                nc.gpsimd.tensor_tensor(rstd2[:], ve2[:], half_neg[:, 0:1], ALU.pow).then_inc(rstd2_done, 1)

            def add_parities(t):
                pool.wait_ge(xz_copied, t + 1)
                if not (isinstance(t, int) and t < 1):
                    pool.wait_ge(q_done, t)
                xz = xzT[:].rearrange("p a b (e k) -> p (a b) e k", e=2)
                nc.gpsimd.tensor_tensor(xT[:].rearrange("p a (b k) -> p (a b) k", b=2),
                                        xz[:, :, 0, :], xz[:, :, 1, :], ALU.add).then_inc(x_added, 1)

            def add_bias(t, par):
                pool.wait_ge(h2_done, t + 1)
                if not (isinstance(t, int) and t < 2):
                    pool.wait_ge(y_set, t - 1)
                nc.gpsimd.tensor_tensor(h2b[par][:], h2[:], fbias_bc[:], ALU.add).then_inc(h2b_done, 1)

            def step(i, par):
                late = not isinstance(i, int)
                if late or i + 2 < T:
                    add_parities(i + 2)
                if late or 0 <= i < T:
                    add_bias(i, par)
                    inv_std(i)

            for i in range(-2, 2):
                step(i, i % 2)
            with pool.Fori(1, T // 2 - 1) as u:
                step(2 * u, 0)
                step(2 * u + 1, 1)
            for i in range(T - 2, T):
                step(i, i % 2)

        @block.vector
        def _(dve):
            def copied(dst, src):
                nc.vector.tensor_copy(dst, src).then_inc(prep_copied, 1)

            for g in range(G):
                dve.wait_ge(prep_pe, g + 1)
                copied(xcatT[:, g, :], bank[4 + g][:, 0:P])
            dve.wait_ge(wh_loaded, 32)
            for r in range(GROUP):
                last = nc.vector.tensor_copy(wh_rep[:, :, r, :], wh_raw[:])
            last.then_inc(rep_done, 1)
            dve.wait_ge(wr_loaded, 48)
            nc.vector.tensor_tensor(br[:], br[:], bo[:], ALU.add).then_inc(bias_joined, 1)
            for r in range(GROUP):
                last = nc.vector.tensor_copy(wr_rep[:, :, r, :], wr_raw[:])
            last.then_inc(rep_done, 1)
            dve.wait_ge(rep_done, 2)
            dve.wait_ge(bias_joined, 1)
            for r in range(GROUP):
                nc.vector.tensor_tensor(wh_rep[:, :, r, PATCH], wh_rep[:, :, r, PATCH], bh[:],
                                        ALU.add).then_inc(rep_biased, 1)
            for r in range(GROUP):
                nc.vector.tensor_tensor(wr_rep[:, :, r, PATCH], wr_rep[:, :, r, PATCH], br[:],
                                        ALU.add).then_inc(rep_biased, 1)
            dve.wait_ge(prep_pe, 5)
            copied(whT[:], bank[0][:])
            dve.wait_ge(prep_pe, 6)
            copied(wrT[:].rearrange("f (p c) -> f c p", c=HALF),
                   bank[1][:, 0:D].rearrange("f (c p) -> f c p", c=HALF))
            for c in range(NC):
                dve.wait_ge(prep_pe, 7 + c)
                copied(woT[:, c, :], bank[4 + c][:, 0:D])


            def spread(dst, g, free, done):
                if not (isinstance(g, int) and g == 0):
                    dve.wait_ge(free, GROUP * g)
                nc.vector.tensor_scalar(dst[:], xcatT[:, bass.ds(g, 1), :].rearrange("p o t -> p (o t)"), 1.0, None,
                                        ALU.mult).then_inc(done, 1)

            def mixed(t):
                dve.wait_ge(h_copied, t + 1)
                nc.vector.bn_stats(stats1[:, bass.ds(t, 1), :].rearrange("p o s -> p (o s)"),
                                   h_all[:, bass.ds(t, 1), :].rearrange("p o d -> p (o d)")).then_inc(stats1_done, 1)

            def group(g, last):
                mixed(GROUP * g)
                mixed(GROUP * g + 1)
                if not last:
                    spread(xg_hid, g + 1, hid_done, xg_hid_set)
                mixed(GROUP * g + 2)
                if not last:
                    spread(xg_res, g + 1, mix_done, xg_res_set)
                mixed(GROUP * g + 3)

            dve.wait_ge(prep_copied, 4)
            spread(xg_hid, 0, hid_done, xg_hid_set)
            spread(xg_res, 0, mix_done, xg_res_set)
            with dve.Fori(0, G - 1) as g:
                group(g, False)
            group(G - 1, True)
            dve.wait_ge(stats1_done, T)
            for t in range(T):
                nc.vector.bn_aggr(mv1[:, t, :], stats1[:, t, :]).then_inc(mv1_done, 1)
            dve.wait_ge(mv1_done, T)
            nc.vector.tensor_scalar(ve1[:], mv1[:, :, 1], EPS, None, ALU.add).then_inc(ve1_done, 1)

            dve.wait_ge(att_loaded, 96)
            dve.wait_ge(ident_loaded, 16)
            for r in range(P // HD):
                nc.vector.tensor_copy(wrep[:, :, r * HD:(r + 1) * HD], wqk[:])
                last = nc.vector.tensor_copy(erep[:, r * HD:(r + 1) * HD], ident[0:HD, 0:HD])
            last.then_inc(rep_done, 1)
            for c in range(HALF):
                dve.wait_ge(prep_pe, 11 + c)
                copied(woutT[:, c, :], bank[4 + c][:, 0:D])
            dve.wait_ge(prep_pe, 13)
            nc.vector.scalar_tensor_tensor(score_w[:], bank[6][:, 0:P], float(D) ** -0.5, blocks[:],
                                           ALU.mult, ALU.mult).then_inc(prep_copied, 1)
            dve.wait_ge(prep_pe, 14)
            nc.vector.tensor_tensor(wv_blocks[:], bank[7][:, 0:P], blocks[:], ALU.mult).then_inc(prep_copied, 1)
            for c in range(HALF):
                dve.wait_ge(prep_pe, 15 + c)
                copied(value_w[:, c, :], bank[4 + c][:, 0:D])
            for c in range(2):
                dve.wait_ge(prep_pe, 17 + c)
                copied(halfway[:, c, :], bank[6 + c][:, 0:D])
            for c in range(HALF):
                dve.wait_ge(prep_pe, 19 + c)
                nc.vector.tensor_scalar(mix_w[:, c, :], bank[c][:, 0:D], 1.0 / D, None,
                                        ALU.mult).then_inc(prep_copied, 1)

            def normalize(t, par):
                if isinstance(t, int) and t < 2:
                    dve.wait_ge(zeros_set, par + 1)
                else:
                    dve.wait_ge(pv_done, t - 1)
                for b in range(2):
                    own = slice(TOK * b, TOK * b + TOK)
                    for e in range(2):
                        src = h_all[own, bass.ds(t, 1), :].rearrange("p o (g e d) -> p (o g) e d", e=2, d=HD)
                        dst = xblk[par][TOK * e:TOK * e + TOK, b, :].rearrange("p (g e d) -> p g e d", e=2, d=HD)
                        last = nc.vector.tensor_scalar(
                            dst[:, :, e, :], src[:, :, e, :],
                            mv1[own, bass.ds(t, 1), 0], rstd1[own, bass.ds(t, 1)],
                            ALU.subtract, ALU.mult)
                last.then_inc(xblk_set, 1)

            def softmax_shift(t):
                def maximum(j):
                    dve.wait_ge(scores_done, QUADS * t + j + 1)
                    nc.vector.tensor_reduce(rowmax[:, j, :], bank[j][:, 0:D].rearrange("p (h k) -> p h k", k=TOK),
                                            AX_X, ALU.max).then_inc(max_done, 1)

                def shift(j):
                    dve.wait_ge(max_done, QUADS * t + j + 1)
                    nc.vector.tensor_tensor(probs[:, j, :].rearrange("p (h k) -> p h k", k=TOK),
                                            bank[j][:, 0:D].rearrange("p (h k) -> p h k", k=TOK),
                                            rowmax[:, j, :].unsqueeze(2).to_broadcast([P, 4, TOK]),
                                            ALU.subtract).then_inc(shifted, 1)

                maximum(0)
                for j in range(1, QUADS):
                    maximum(j)
                    shift(j - 1)
                shift(QUADS - 1)

            def divide(t):
                dve.wait_ge(pv_done, t + 1)
                nc.vector.reciprocal(inv_sum[:], bank[7][:, D:2 * D]).then_inc(inv_done, 1)
                dve.wait_ge(inv_done, t + 1)
                nc.vector.tensor_tensor(onT[:].rearrange("p a t -> p (a t)"), bank[7][:, 0:D], inv_sum[:],
                                        ALU.mult).then_inc(on_set, 1)

            def residual(t, par, finish_before):
                dve.wait_ge(proj_done, t + 1)
                if not (isinstance(t, int) and t < 1):
                    dve.wait_ge(h2b_done, t)
                nc.vector.tensor_tensor(h2[:], bank[6][:, 0:D],
                                        hb_all[:, bass.ds(t, 1), :].rearrange("p o d -> p (o d)"),
                                        ALU.add).then_inc(h2_done, 1)
                dve.wait_ge(h2_done, t + 1)
                nc.vector.bn_stats(stats2[:], h2[:]).then_inc(stats2_done, 1)
                dve.wait_ge(stats2_done, t + 1)
                if finish_before:
                    finish(t - 1, 1 - par)
                nc.vector.bn_aggr(mv2[:], stats2[:]).then_inc(mv2_done, 1)
                dve.wait_ge(mv2_done, t + 1)
                nc.vector.tensor_scalar(ve2[:], mv2[:, 1:2], EPS, None, ALU.add).then_inc(ve2_done, 1)

            def finish(t, par):
                dve.wait_ge(freq_done, t + 1)
                dve.wait_ge(h2b_done, t + 1)
                if not (isinstance(t, int) and t < 2):
                    dve.wait_ge(y_stored[par], 16 * (t // 2) if isinstance(t, int) else (t - par) * 8)
                nc.vector.tensor_tensor(y[par][:], bank[7][:, 0:D], h2b[par][:], ALU.add).then_inc(y_set, 1)

            def norm2(t):
                dve.wait_ge(rstd2_done, t + 1)
                nc.vector.tensor_scalar(xh2[:], h2[:], mv2[:, 0:1], rstd2[:, 0:1],
                                        ALU.subtract, ALU.mult).then_inc(xh2_set, 1)

            def step(i, par):
                late = not isinstance(i, int)
                if late or 0 <= i + 1 < T:
                    softmax_shift(i + 1)
                if late or 0 <= i < T:
                    divide(i)
                if late or i + 2 < T:
                    normalize(i + 2, par)
                if late or 0 <= i < T:
                    residual(i, par, late or 0 <= i - 1)
                    norm2(i)
                elif i == T:
                    finish(i - 1, 1 - par)

            dve.wait_ge(rstd1_done, 1)
            dve.wait_ge(hb_done, G)
            for i in range(-2, 2):
                step(i, i % 2)
            with dve.Fori(1, T // 2 - 1) as u:
                step(2 * u, 0)
                step(2 * u + 1, 1)
            for i in range(T - 2, T + 1):
                step(i, i % 2)

        @block.tensor
        def _(pe):
            pe.wait_ge(ident_loaded, 16)
            pe.wait_ge(ones_set, 1)
            pe.wait_ge(x_loaded, 16 * G)
            for g in range(G):
                pe.transpose(bank[4 + g][:, 0:P], xcat[:, g * GROUP:(g + 1) * GROUP, :].rearrange("p t f -> p (t f)"),
                             ident[:]).then_inc(prep_pe, 1)
            pe.wait_ge(rep_biased, 2 * GROUP)
            for c in range(NC):
                last = pe.transpose(bank[0][:, c * P:(c + 1) * P], wh_rep[:, c, :, :].rearrange("p r f -> p (r f)"),
                                    ident[:])
            last.then_inc(prep_pe, 1)
            for c in range(HALF):
                last = pe.transpose(bank[1][:, c * P:(c + 1) * P], wr_rep[:, c, :, :].rearrange("p r f -> p (r f)"),
                                    ident[:])
            last.then_inc(prep_pe, 1)
            pe.wait_ge(wo_loaded, 16)
            for c in range(NC):
                pe.wait_ge(prep_copied, c + 1)
                for a2 in range(HALF):
                    last = pe.transpose(bank[4 + c][:, a2 * P:(a2 + 1) * P], wo_raw[:, a2, bass.ds(c, P, step=NC)],
                                        ident[:])
                last.then_inc(prep_pe, 1)

            def hidden(t, quad):
                par = quad % 2
                if quad == 0:
                    pe.wait_ge(xg_hid_set, t // GROUP + 1 if isinstance(t, int) else (t + GROUP) // GROUP)
                if not (isinstance(t, int) and t < 2):
                    pe.wait_ge(silu_done, t - 1)
                rows32 = slice(F * quad, F * quad + F)
                for c in range(NC):
                    last = pe.matmul(bank[par][:, c * P:(c + 1) * P], whT[rows32, c * P:(c + 1) * P],
                                     xg_hid[rows32, :], start=True, stop=True)
                last.then_inc(hid_done, 1)

            def mix(t, quad):
                par = quad % 2
                if quad == 0:
                    pe.wait_ge(xg_res_set, t // GROUP + 1 if isinstance(t, int) else (t + GROUP) // GROUP)
                pe.wait_ge(silu_done, t + 1)
                if not (isinstance(t, int) and t < 2):
                    pe.wait_ge(h_copied, t - 1)
                rows32 = slice(F * quad, F * quad + F)
                for c in range(NC):
                    pe.matmul(bank[2 + par][:, 0:D], hidT[:, par, c * P:(c + 1) * P], woT[:, c, :],
                              start=(c == 0), stop=False)
                pe.matmul(bank[2 + par][:, 0:D], xg_res[rows32, :], wrT[rows32, :],
                          start=False, stop=True).then_inc(mix_done, 1)

            pe.wait_ge(prep_copied, 10)
            hidden(0, 0)
            for t in range(GROUP):
                hidden(t + 1, (t + 1) % GROUP)
                mix(t, t)
            with pe.Fori(1, G - 1) as g:
                for q in range(GROUP):
                    hidden(GROUP * g + q + 1, (q + 1) % GROUP)
                    mix(GROUP * g + q, q)
            for t in range(T - GROUP, T):
                if t + 1 < T:
                    hidden(t + 1, (t + 1) % GROUP)
                mix(t, t % GROUP)

            pe.wait_ge(att_loaded, 96)
            for c in range(HALF):
                for a2 in range(HALF):
                    last = pe.transpose(bank[4 + c][:, a2 * P:(a2 + 1) * P], wout_raw[:, a2, c * P:(c + 1) * P],
                                        ident[:])
                last.then_inc(prep_pe, 1)
            pe.wait_ge(rep_done, 3)
            pe.matmul(bank[6][:, 0:P], wrep[:, 0, :], wrep[:, 1, :], start=True, stop=True).then_inc(prep_pe, 1)
            pe.matmul(bank[7][:, 0:P], erep[:], wrep[:, 2, :], start=True, stop=True).then_inc(prep_pe, 1)
            pe.wait_ge(prep_copied, 14)
            for c in range(HALF):
                pe.matmul(bank[4 + c][:, 0:D], wv_blocks[:], woutT[:, c, :], start=True,
                          stop=True).then_inc(prep_pe, 1)
            pe.wait_ge(folds, 4)
            for c in range(2):
                pe.matmul(bank[6 + c][:, 0:D], cols[:, 2 * c, :], cosine[:], start=True, stop=False)
                pe.matmul(bank[6 + c][:, 0:D], cols[:, 2 * c + 1, :], sine[:], start=False,
                          stop=True).then_inc(prep_pe, 1)
            pe.wait_ge(prep_copied, 18)
            for c in range(HALF):
                pe.matmul(bank[c][:, 0:D], halfway[:, 0, c * P:(c + 1) * P], cosine[:], start=True, stop=False)
                pe.matmul(bank[c][:, 0:D], halfway[:, 1, c * P:(c + 1) * P], sine[:], start=False,
                          stop=True).then_inc(prep_pe, 1)
            pe.wait_ge(prep_copied, 20)

            def scores(t):
                pe.wait_ge(q_copied, t + 1)
                for j in range(QUADS):
                    if not (isinstance(t, int) and t < 1):
                        pe.wait_ge(shifted, QUADS * (t - 1) + j + 1)
                    rows32 = slice(32 * j, 32 * j + 32)
                    for half in range(HALF):
                        for b in range(2):
                            last = pe.matmul(bank[j][TOK * b:TOK * b + TOK, half * P:(half + 1) * P],
                                             qT[rows32, half, TOK * b:TOK * b + TOK], xzT[rows32, half, b, :],
                                             start=True, stop=True)
                    last.then_inc(scores_done, 1)

            def weigh(t, par):
                pe.wait_ge(p_copied, 2 * (t + 1))
                if not (isinstance(t, int) and t < 2):
                    pe.wait_ge(y_set, t - 1)
                for half in range(HALF):
                    for b in range(2):
                        for j in range(QUADS):
                            pe.matmul(bank[7][32 * j:32 * j + 32, half * P + TOK * b:half * P + TOK * (b + 1)],
                                      xblk[par][:, b, half * P + 32 * j:half * P + 32 * j + 32],
                                      pT[:, 2 * j + half, TOK * b:TOK * b + TOK], start=True, stop=True)
                for half in range(HALF):
                    for j in range(QUADS):
                        last = pe.matmul(bank[7][32 * j:32 * j + 32, D + half * P:D + (half + 1) * P],
                                         head_sum[:], pT[:, 2 * j + half, :], start=True, stop=True)
                last.then_inc(pv_done, 1)

            def turn_xh2(t):
                pe.wait_ge(xh2_set, t + 1)
                for half in range(HALF):
                    last = pe.transpose(bank[5][:, half * P:(half + 1) * P], xh2[:, half * P:(half + 1) * P], ident[:])
                last.then_inc(xh2_turned, 1)

            def project(t):
                pe.wait_ge(on_set, t + 1)
                for half in range(HALF):
                    last = pe.matmul(bank[6][:, 0:D], onT[:, half, :], value_w[:, half, :],
                                     start=(half == 0), stop=(half == HALF - 1))
                last.then_inc(proj_done, 1)

            def turn_xz(t, par):
                pe.wait_ge(xblk_set, t + 1)
                for half in range(HALF):
                    for b in range(2):
                        k = (2 * half + b) * P
                        last = pe.transpose(bank[4][:, k:k + P], xblk[par][:, b, half * P:(half + 1) * P], ident[:])
                last.then_inc(xz_turned, 1)

            def mix_freq(t):
                pe.wait_ge(xh2_copied, t + 1)
                for half in range(HALF):
                    last = pe.matmul(bank[7][:, 0:D], xh2T[:, half, :], mix_w[:, half, :],
                                     start=(half == 0), stop=(half == HALF - 1))
                last.then_inc(freq_done, 1)

            def turn_p(t, part):
                pe.wait_ge(exp_done, QUADS * t + 2 * part + 2)
                if part == 1 and not (isinstance(t, int) and t < 1):
                    pe.wait_ge(h2_done, t)
                for k in range(4):
                    j, half = 2 * part + k // 2, k % 2
                    last = pe.transpose(bank[5 + part][:, k * P:(k + 1) * P], probs[:, j, half * P:(half + 1) * P],
                                        ident[:])
                last.then_inc(p_turned, 1)

            def query(t):
                pe.wait_ge(x_added, t + 1)
                for half in range(HALF):
                    last = pe.matmul(bank[4][:, half * P:(half + 1) * P], score_w[:], xT[:, half, :],
                                     start=True, stop=True)
                last.then_inc(q_done, 1)

            def step(i, par):
                late = not isinstance(i, int)
                if late or 0 <= i + 1 < T:
                    scores(i + 1)
                if late or 0 <= i < T:
                    weigh(i, par)
                if late or 0 <= i - 1:
                    turn_xh2(i - 1)
                if late or 0 <= i < T:
                    project(i)
                if late or i + 2 < T:
                    turn_xz(i + 2, par)
                if late or 0 <= i - 1:
                    mix_freq(i - 1)
                if late or 0 <= i + 1 < T:
                    turn_p(i + 1, 0)
                if late or i + 2 < T:
                    query(i + 2)
                if late or 0 <= i + 1 < T:
                    turn_p(i + 1, 1)

            for i in range(-2, 2):
                step(i, i % 2)
            with pe.Fori(1, T // 2 - 1) as u:
                step(2 * u, 0)
                step(2 * u + 1, 1)
            for i in range(T - 2, T + 1):
                step(i, i % 2)


_INS = {
    "x": "x", "L0_tok_W_h": "W_h", "L0_tok_b_h": "b_h", "L0_tok_W_o": "W_o", "L0_tok_b_o": "b_o",
    "L0_tok_W_r": "W_r", "L0_tok_b_r": "b_r", "L0_attn_Wq": "Wq", "L0_attn_Wk": "Wk", "L0_attn_Wv": "Wv",
    "L0_attn_W_out": "W_out", "L0_attn_b_out": "b_out", "L0_ffn_w_freq_real": "wr", "L0_ffn_w_freq_imag": "wi",
    "L0_ffn_bias": "bias",
}


def kernel(**inputs):
    import concourse.bacc as _bacc
    from concourse.bass_utils import run_bass_kernel_spmd as _run

    nc = _bacc.Bacc("TRN2", target_bir_lowering=False, num_devices=1)
    arrays, args = {}, {}
    data = {short: np.asarray(inputs[name]) for name, short in _INS.items()}
    for short in ("wr", "wi"):
        data[short] = data[short][FOLDED][:, FOLDED]
    data.update(launch_constants())
    for short, v in data.items():
        v = np.ascontiguousarray(v)
        arrays[f"in_{short}"] = v
        args[short] = nc.dram_tensor(f"in_{short}", v.shape, mybir.dt.from_np(v.dtype), kind="ExternalInput").ap()
    out = nc.dram_tensor("out_0", (BATCH, TOK, D), F32, kind="ExternalOutput").ap()
    audio_tower_kernel(nc, args, out)
    r = _run(nc, [arrays], core_ids=[0])
    return r.results[0]["out_0"]
```

```python
from contextlib import ExitStack

import concourse.bass as bass
import numpy as np
from concourse import mybir

F32 = mybir.dt.float32
BF16 = mybir.dt.bfloat16
ALU = mybir.AluOpType
ACT = mybir.ActivationFunctionType
AX_X = mybir.AxisListType.X

P = 128
BATCH, LENGTH = 32, 1024
PATCH = 16
TOK = LENGTH // PATCH
TERMS = 6
BIAS = TERMS * PATCH
HID = 512
NC = HID // P
D = 256
HEADS, HD = 16, 16
T = BATCH * TOK // P
GROUP = 4
HALF = D // P
QUADS = 4
EPS = 1e-5


def launch_constants():
    k = np.arange(P)[:, None].astype(np.float64)
    n = np.arange(D)[None, :].astype(np.float64)
    cosine = np.cos(2 * np.pi * k * n / D)
    sine = np.sin(2 * np.pi * k * n / D)
    sine[0] = np.cos(np.pi * n[0])
    r = np.arange(P)
    head_blocks = (r[:, None] // HD == r[None, :] // HD).astype(np.float32)
    parity = (np.stack([r // HD % 2, r // HD % 2, r // TOK, r // TOK], 1) == [0, 1, 0, 1]).astype(np.float32)
    return {
        "identity": np.eye(P, dtype=np.float32),
        "head_blocks": head_blocks,
        "parity": parity,
        "cosine": cosine.astype(np.float32),
        "sine": sine.astype(np.float32),
    }


FOLDED = np.concatenate([np.arange(P), [P], np.arange(D - 1, P, -1)])


def audio_tower_kernel(nc, a, out):
    with ExitStack() as ctx:
        def sb(name, shape, dtype=F32):
            return ctx.enter_context(nc.sbuf_tensor(name, shape, dtype))

        def sem(name):
            return ctx.enter_context(nc.semaphore(name))

        ident = sb("ident", [P, P])
        ident16 = sb("ident16", [P, P], BF16)
        blocks = sb("blocks", [P, P])
        parity = sb("parity_sb", [P, 4])
        cosine = sb("cosine_sb", [P, D])
        sine = sb("sine_sb", [P, D])
        bh = sb("bh", [P, NC])
        br = sb("br", [P, HALF])
        bo = sb("bo", [P, HALF])
        wf_raw = sb("wf_raw", [P, NC + HALF, 2 * PATCH])
        wb = sb("wb", [P, NC + HALF, PATCH + 1])
        wb_part = [sb(f"wb_part{i}", [P, NC + HALF, PATCH + 1], BF16) for i in range(3)]
        wb_rest = [sb(f"wb_rest{i}", [P, NC + HALF, PATCH + 1]) for i in range(2)]
        w_terms = sb("w_terms", [P, NC + HALF, P], BF16)
        w_termsT = sb("w_termsT", [P, (NC + HALF) * P], BF16)
        wr_termsT = sb("wr_termsT", [P, D], BF16)
        wo_raw = sb("wo_raw", [P, HALF, HID])
        wout_raw = sb("wout_raw", [P, HALF, D])
        woT = sb("woT", [P, NC, D])
        woutT = sb("woutT", [P, HALF, D])
        wqk = sb("wqk", [HD, 3, HD])
        wrep = sb("wrep", [HD, 3, P])
        erep = sb("erep", [HD, P])
        score_w = sb("score_w", [P, P])
        wv_blocks = sb("wv_blocks", [P, P])
        value_w = sb("value_w", [P, HALF, D])
        fr = sb("fr", [P, 2, D])
        fi = sb("fi", [P, 2, D])
        rows = sb("rows", [P, 4, D])
        cols = sb("cols", [P, 4, P])
        halfway = sb("halfway", [P, 2, D])
        mix_w = sb("mix_w", [P, HALF, D])
        bout_bc = sb("bout_bc", [P, D])
        fbias_bc = sb("fbias_bc", [P, D])
        xs = sb("xs", [P, T, PATCH])
        x_part = [sb(f"x_part{i}", [P, T, PATCH], BF16) for i in range(3)]
        x_rest = [sb(f"x_rest{i}", [P, T, PATCH]) for i in range(2)]
        x_terms = sb("x_terms", [P, T, P], BF16)
        x_termsT = sb("x_termsT", [P, T * P], BF16)
        hidT = sb("hidT", [P, 2, HID])
        h_all = sb("h_all", [P, T, D])
        hb_all = sb("hb_all", [P, T, D])
        stats1 = sb("stats1", [P, T, 6])
        mv1 = sb("mv1", [P, T, 2])
        ve1 = sb("ve1", [P, T])
        rstd1 = sb("rstd1", [P, T])
        shift1 = sb("shift1", [P, T])
        half_neg = sb("half_neg", [P, T])
        xh = [sb(f"xh{i}", [P, D]) for i in range(2)]
        xblk = [sb(f"xblk{i}", [P, 2, D]) for i in range(2)]
        xT = sb("xT", [P, D])
        xzT = sb("xzT", [P, 2 * HALF, 2, TOK])
        qT = sb("qT", [P, HALF, P])
        rowmax = sb("rowmax", [P, QUADS, 4])
        probs = sb("probs", [P, QUADS, D])
        half_sums = sb("half_sums", [P, QUADS, 4, TOK // 2])
        sums = sb("sums", [P, QUADS, HALF, 2])
        inv_sum = sb("inv_sum", [P, QUADS, HALF, 2])
        inv_rows = sb("inv_rows", [P, HALF, 2 * QUADS, HD])
        pT = sb("pT", [P, 2 * QUADS, P])
        sideT = sb("sideT", [P, 2 * D])
        onT = sb("onT", [P, HALF, P])
        h2 = sb("h2", [P, D])
        h2b = [sb(f"h2b{i}", [P, D]) for i in range(2)]
        stats2 = sb("stats2", [P, 6])
        mv2 = sb("mv2", [P, 2])
        ve2 = sb("ve2", [P, 1])
        rstd2 = sb("rstd2", [P, 1])
        xh2 = sb("xh2", [P, D])
        y = [sb(f"y{i}", [P, D]) for i in range(2)]

        bank = [ctx.enter_context(nc.psum_tensor(f"bank{i}", [P, 512], F32)) for i in range(8)]
        bank16 = [b[:].bitcast(BF16) for b in bank]
        HID_BANK, MIX_BANK = (0, 1), (5, 6)
        T1_BANK, SIDE_BANK, PROJ_BANK, PV_BANK = 4, 5, 6, 7

        x_loaded, w_loaded, wo_loaded = sem("x_loaded"), sem("w_loaded"), sem("wo_loaded")
        ident_loaded, att_loaded, wout_loaded, freq_loaded, bias_loaded = (
            sem("ident_loaded"), sem("att_loaded"), sem("wout_loaded"), sem("freq_loaded"), sem("bias_loaded"))
        const_set, wb_set, wb_split, x_split = sem("const_set"), sem("wb_set"), sem("wb_split"), sem("x_split")
        w_placed, x_placed = sem("w_placed"), sem("x_placed")
        w_turned, w_copied, x_turned, x_copied = sem("w_turned"), sem("w_copied"), sem("x_turned"), sem("x_copied")
        wo_turned, wo_copied = sem("wo_turned"), sem("wo_copied")
        reps_set, small_done, small_copied = sem("reps_set"), sem("small_done"), sem("small_copied")
        wout_turned, wout_copied, value_done, value_copied = (
            sem("wout_turned"), sem("wout_copied"), sem("value_done"), sem("value_copied"))
        rows_set, cols_set = sem("rows_set"), sem("cols_set")
        halfway_done, halfway_copied, mixw_done, mixw_copied = (
            sem("halfway_done"), sem("halfway_copied"), sem("mixw_done"), sem("mixw_copied"))
        hid_done, silu_done, mix_done = sem("hid_done"), sem("silu_done"), sem("mix_done")
        h_copied, hb_done, stats1_done, mv1_done, ve1_done, rstd1_done, shift1_done = (
            sem("h_copied"), sem("hb_done"), sem("stats1_done"), sem("mv1_done"), sem("ve1_done"),
            sem("rstd1_done"), sem("shift1_done"))
        xh_set, x1_turned, xT_copied, xzT_copied = sem("xh_set"), sem("x1_turned"), sem("xT_copied"), sem("xzT_copied")
        xblk_same, xblk_crossed = sem("xblk_same"), sem("xblk_crossed")
        q_done, q_copied = sem("q_done"), sem("q_copied")
        scores_done, max_done, shifted, exp_done = sem("scores_done"), sem("max_done"), sem("shifted"), sem("exp_done")
        half_sums_done, sums_done, inv_done, inv_spread = (
            sem("half_sums_done"), sem("sums_done"), sem("inv_done"), sem("inv_spread"))
        side_turned, side_copied = sem("side_turned"), sem("side_copied")
        p_turned, p_copied, pv_done, on_set = sem("p_turned"), sem("p_copied"), sem("pv_done"), sem("on_set")
        proj_done, h2_done = sem("proj_done"), sem("h2_done")
        stats2_done, mv2_done, ve2_done, rstd2_done = sem("stats2_done"), sem("mv2_done"), sem("ve2_done"), sem("rstd2_done")
        h2b_done, xh2_set, freq_done, y_set = sem("h2b_done"), sem("xh2_set"), sem("freq_done"), sem("y_set")
        y_stored = [sem("y_stored0"), sem("y_stored1")]

        x_tok = a["x"].rearrange("b (n f) -> (b n) f", f=PATCH).rearrange("(t p) f -> p t f", p=P)
        out_tok = out.rearrange("b n d -> (b n) d").rearrange("(t p) d -> p t d", p=P)

        def tile_of(tensor, t):
            return tensor[:, bass.ds(t, 1), :].rearrange("p o n -> p (o n)")

        def first(t, n):
            return isinstance(t, int) and t < n

        def has(t):
            return not isinstance(t, int) or 0 <= t < T

        X_PARTS = ((0, 0, 3), (1, 3, 2), (2, 5, 1))
        W_PARTS = (0, 1, 2, 0, 1, 0)

        block = ctx.enter_context(nc.Block())

        @block.sync
        def _(sp):
            for g in range(2):
                tiles = slice(g * T // 2, (g + 1) * T // 2)
                sp.dma_start(xs[:, tiles, :], x_tok[:, tiles, :]).then_inc(x_loaded, 16)
            sp.dma_start(wo_raw[:], a["W_o"].rearrange("(c p) i -> p c i", p=P)).then_inc(wo_loaded, 16)
            for i, name in enumerate(("Wq", "Wk", "Wv")):
                sp.dma_start(wqk[:, i, :], a[name]).then_inc(att_loaded, 16)
            sp.dma_start(blocks[:], a["head_blocks"]).then_inc(att_loaded, 16)
            sp.dma_start(parity[:], a["parity"]).then_inc(att_loaded, 16)
            for name, dst in (("wr", fr), ("wi", fi)):
                sp.dma_start(dst[:], a[name].rearrange("(c p) n -> p c n", p=P)).then_inc(freq_loaded, 16)

            def store(t, par):
                sp.wait_ge(y_set, t + 1)
                sp.dma_start(tile_of(out_tok, t), y[par][:]).then_inc(y_stored[par], 16)

            with sp.Fori(0, T // 2) as u:
                store(2 * u, 0)
                store(2 * u + 1, 1)
            for par in range(2):
                sp.wait_ge(y_stored[par], 16 * (T // 2))

        @block.scalar
        def _(act):
            act.dma_start(wf_raw[:, 0:NC, :], a["W_h"].rearrange("(p c) f -> p c f", p=P)).then_inc(w_loaded, 16)
            act.dma_start(wf_raw[:, NC:, :], a["W_r"].rearrange("(p c) f -> p c f", p=P)).then_inc(w_loaded, 16)
            act.dma_start(bh[:], a["b_h"].rearrange("(p c) -> p c", p=P)).then_inc(w_loaded, 16)
            act.dma_start(br[:], a["b_r"].rearrange("(p c) -> p c", p=P)).then_inc(w_loaded, 16)
            act.dma_start(bo[:], a["b_o"].rearrange("(p c) -> p c", p=P)).then_inc(w_loaded, 16)
            act.dma_start(ident[:], a["identity"]).then_inc(ident_loaded, 16)
            act.dma_start(bout_bc[:], a["b_out"].partition_broadcast(P)).then_inc(bias_loaded, 16)
            act.dma_start(cosine[:], a["cosine"]).then_inc(freq_loaded, 16)
            act.dma_start(sine[:], a["sine"]).then_inc(freq_loaded, 16)
            act.dma_start(wout_raw[:], a["W_out"].rearrange("(c p) i -> p c i", p=P)).then_inc(wout_loaded, 16)
            act.dma_start(fbias_bc[:], a["bias"].partition_broadcast(P)).then_inc(bias_loaded, 16)

            act.wait_ge(const_set, 3)
            for part, slot, n in X_PARTS:
                act.wait_ge(x_split, 1 + 2 * part)
                nc.scalar.activation(
                    x_terms[:, :, slot * PATCH:(slot + n) * PATCH].rearrange("p t (n f) -> p t n f", n=n),
                    x_part[part][:].unsqueeze(2).to_broadcast([P, T, n, PATCH]), ACT.Copy).then_inc(x_placed, 1)
            for c in range(NC):
                act.wait_ge(wo_turned, c + 1)
                nc.scalar.activation(woT[:, c, :], bank[2 + c][:, 0:D], ACT.Copy).then_inc(wo_copied, 1)
            for g in range(2):
                act.wait_ge(x_turned, g + 1)
                nc.scalar.activation(x_termsT[:, g * 1024:(g + 1) * 1024], bank16[6 + g], ACT.Copy).then_inc(x_copied, 1)

            def silu(t, par):
                act.wait_ge(hid_done, t + 1)
                if not first(t, 2):
                    act.wait_ge(mix_done, t - 1)
                nc.scalar.activation(hidT[:, par, :], bank[HID_BANK[par]][:], ACT.Silu).then_inc(silu_done, 1)

            def copy_h(t, par):
                act.wait_ge(mix_done, t + 1)
                nc.scalar.activation(tile_of(h_all, t), bank[MIX_BANK[par]][:, 0:D], ACT.Copy).then_inc(h_copied, 1)

            silu(0, 0)
            silu(1, 1)
            copy_h(0, 0)
            silu(2, 0)
            copy_h(1, 1)
            with act.Fori(1, T // 2 - 1) as u:
                silu(2 * u + 1, 1)
                copy_h(2 * u, 0)
                silu(2 * u + 2, 0)
                copy_h(2 * u + 1, 1)
            silu(T - 1, 1)
            copy_h(T - 2, 0)
            copy_h(T - 1, 1)

            def normalize(t, par):
                act.wait_ge(shift1_done, (t // (T // 2) + 1) if isinstance(t, int) else 2)
                if not first(t, 2):
                    act.wait_ge(xblk_same, t - 1)
                    act.wait_ge(xblk_crossed, t - 1)
                nc.scalar.activation(xh[par][:], tile_of(h_all, t), ACT.Identity,
                                     bias=shift1[:, bass.ds(t, 1)], scale=rstd1[:, bass.ds(t, 1)]).then_inc(xh_set, 1)

            def spread_inverse(t):
                act.wait_ge(inv_done, t + 1)
                for half in range(HALF):
                    last = nc.scalar.activation(
                        inv_rows[:, half, :, :].rearrange("p (q e) d -> p q e d", e=2),
                        inv_sum[:, :, half, :].unsqueeze(3).to_broadcast([P, QUADS, 2, HD]), ACT.Copy)
                last.then_inc(inv_spread, 1)

            def exponent(t, j):
                act.wait_ge(shifted, QUADS * t + j + 1)
                nc.scalar.activation(probs[:, j, :], probs[:, j, :], ACT.Exp).then_inc(exp_done, 1)

            def copy_side(lo, hi, n):
                act.wait_ge(side_turned, n)
                nc.scalar.activation(sideT[:, lo:hi], bank[SIDE_BANK][:, lo:hi], ACT.Copy).then_inc(side_copied, 1)

            def copy_x(t):
                act.wait_ge(x1_turned, t + 1)
                nc.scalar.activation(xT[:], bank[T1_BANK][:, 0:D], ACT.Copy).then_inc(xT_copied, 1)
                for e in range(2):
                    nc.scalar.activation(xzT[:, :, e, :], bank[T1_BANK][:, 0:D].rearrange("p (g k) -> p g k", k=TOK),
                                         ACT.Copy, scale=parity[:, e:e + 1]).then_inc(xzT_copied, 1)

            def copy_q(t):
                act.wait_ge(q_done, t + 1)
                nc.scalar.activation(qT[:].rearrange("p a t -> p (a t)"), bank[PV_BANK][:, 0:D],
                                     ACT.Copy).then_inc(q_copied, 1)

            def copy_p(t, part):
                act.wait_ge(p_turned, 2 * t + part + 1)
                nc.scalar.activation(pT[:, 4 * part:4 * part + 4, :].rearrange("p a t -> p (a t)"),
                                     bank[(SIDE_BANK, T1_BANK)[part]][:], ACT.Copy).then_inc(p_copied, 1)

            def step(i, par):
                if has(i):
                    spread_inverse(i)
                if has(i + 2):
                    normalize(i + 2, par)
                if has(i) or has(i - 1):
                    copy_side(0 if has(i - 1) else D, 2 * D if has(i) else D, i + 1)
                if has(i + 1):
                    exponent(i + 1, 0)
                    exponent(i + 1, 1)
                    exponent(i + 1, 2)
                    exponent(i + 1, 3)
                if has(i + 2):
                    copy_x(i + 2)
                    copy_q(i + 2)
                if has(i + 1):
                    copy_p(i + 1, 0)
                    copy_p(i + 1, 1)

            act.wait_ge(att_loaded, 80)
            normalize(0, 0)
            for c in range(HALF):
                act.wait_ge(wout_turned, c + 1)
                nc.scalar.activation(woutT[:, c, :], bank[c][:, 0:D], ACT.Copy).then_inc(wout_copied, 1)
            for c in range(2):
                act.wait_ge(halfway_done, c + 1)
                nc.scalar.activation(halfway[:, c, :], bank[2 + c][:, 0:D], ACT.Copy).then_inc(halfway_copied, 1)
            copy_x(0)
            for c in range(HALF):
                act.wait_ge(value_done, c + 1)
                nc.scalar.activation(value_w[:, c, :], bank[c][:, 0:D], ACT.Copy).then_inc(value_copied, 1)
            copy_q(0)
            for c in range(HALF):
                act.wait_ge(mixw_done, c + 1)
                nc.scalar.activation(mix_w[:, c, :], bank[2 + c][:, 0:D], ACT.Copy, scale=1.0 / D).then_inc(mixw_copied, 1)
            for i in range(-1, 2):
                step(i, i % 2)
            with act.Fori(1, T // 2 - 1) as u:
                step(2 * u, 0)
                step(2 * u + 1, 1)
            for i in range(T - 2, T + 1):
                step(i, i % 2)

        @block.gpsimd
        def _(pool):
            nc.gpsimd.memset(w_terms[:], 0.0).then_inc(const_set, 1)
            nc.gpsimd.memset(x_terms[:, :, BIAS + 3:P], 0.0).then_inc(const_set, 1)
            nc.gpsimd.memset(x_terms[:, :, BIAS:BIAS + 3], 1.0).then_inc(const_set, 1)
            nc.gpsimd.memset(half_neg[:], -0.5).then_inc(const_set, 1)
            for i in range(2):
                nc.gpsimd.memset(xblk[i][:], 0.0).then_inc(const_set, 1)

            pool.wait_ge(const_set, 6)
            pool.wait_ge(bias_loaded, 32)

            def residual_bias(g):
                tiles = slice(GROUP * g, GROUP * (g + 1))
                pool.wait_ge(h_copied, GROUP * (g + 1))
                nc.gpsimd.tensor_tensor(hb_all[:, tiles, :], h_all[:, tiles, :],
                                        bout_bc[:].unsqueeze(1).to_broadcast([P, GROUP, D]),
                                        ALU.add).then_inc(hb_done, 1)

            def inv_std1(half):
                tiles = slice(T // 2 * half, T // 2 * (half + 1))
                pool.wait_ge(ve1_done, half + 1)
                nc.gpsimd.tensor_tensor(rstd1[:, tiles], ve1[:, tiles], half_neg[:, tiles],
                                        ALU.pow).then_inc(rstd1_done, 1)

            residual_bias(0)
            residual_bias(1)
            inv_std1(0)
            residual_bias(2)
            inv_std1(1)
            residual_bias(3)

            def halve_sums(t, part):
                quads = slice(2 * part, 2 * part + 2)
                pr = probs[:, quads, :].rearrange("p q (h s k) -> p (q h) s k", s=2, k=TOK // 2)
                nc.gpsimd.tensor_tensor(half_sums[:, quads, :, :].rearrange("p q h k -> p (q h) k"),
                                        pr[:, :, 0, :], pr[:, :, 1, :], ALU.add).then_inc(half_sums_done, 1)

            def place_same(par):
                for b in range(2):
                    last = nc.gpsimd.tensor_scalar(
                        xblk[par][:, b, :].rearrange("p (g e d) -> p g e d", e=2, d=HD)[:, :, b, :],
                        xh[par][:].rearrange("p (g e d) -> p g e d", e=2, d=HD)[:, :, b, :],
                        parity[:, 2 + b:3 + b], 1.0, ALU.mult, ALU.mult)
                last.then_inc(xblk_same, 1)

            def inv_std2(t):
                pool.wait_ge(ve2_done, t + 1)
                if not first(t, 1):
                    pool.wait_ge(xh2_set, t)
                nc.gpsimd.tensor_tensor(rstd2[:], ve2[:], half_neg[:, 0:1], ALU.pow).then_inc(rstd2_done, 1)

            def add_bias(t, par):
                if not first(t, 2):
                    pool.wait_ge(y_set, t - 1)
                nc.gpsimd.tensor_tensor(h2b[par][:], h2[:], fbias_bc[:], ALU.add).then_inc(h2b_done, 1)

            def step(i, par):
                if has(i + 1):
                    pool.wait_ge(exp_done, QUADS * (i + 1) + 2)
                    if not first(i + 1, 1):
                        pool.wait_ge(sums_done, i + 1)
                    halve_sums(i + 1, 0)
                    if has(i + 2):
                        pool.wait_ge(xh_set, i + 3)
                        if has(i):
                            pool.wait_ge(pv_done, i + 1)
                    pool.wait_ge(exp_done, QUADS * (i + 1) + 4)
                    halve_sums(i + 1, 1)
                if has(i + 2):
                    place_same(par)
                if has(i):
                    inv_std2(i)
                    add_bias(i, par)

            pool.wait_ge(xh_set, 1)
            place_same(0)
            for i in range(-1, 2):
                step(i, i % 2)
            with pool.Fori(1, T // 2 - 1) as u:
                step(2 * u, 0)
                step(2 * u + 1, 1)
            for i in range(T - 2, T):
                step(i, i % 2)

        @block.vector
        def _(dve):
            dve.wait_ge(w_loaded, 80)
            nc.vector.tensor_copy(wb[:, :, 0:PATCH], wf_raw[:, :, 0:PATCH]).then_inc(wb_set, 1)
            nc.vector.tensor_reduce(wb[:, :, PATCH], wf_raw[:, :, PATCH:], AX_X, ALU.add).then_inc(wb_set, 1)
            nc.vector.tensor_tensor(br[:], br[:], bo[:], ALU.add).then_inc(wb_set, 1)
            dve.wait_ge(wb_set, 3)
            nc.vector.tensor_tensor(wb[:, 0:NC, PATCH], wb[:, 0:NC, PATCH], bh[:], ALU.add).then_inc(wb_set, 1)
            nc.vector.tensor_tensor(wb[:, NC:, PATCH], wb[:, NC:, PATCH], br[:], ALU.add).then_inc(wb_set, 1)

            def split(src, part, rest, done):
                nc.vector.tensor_copy(part[0][:], src[:]).then_inc(done, 1)
                dve.wait_ge(done, 1)
                nc.vector.tensor_tensor(rest[0][:], src[:], part[0][:], ALU.subtract).then_inc(done, 1)
                dve.wait_ge(done, 2)
                nc.vector.tensor_copy(part[1][:], rest[0][:]).then_inc(done, 1)
                dve.wait_ge(done, 3)
                nc.vector.tensor_tensor(rest[1][:], rest[0][:], part[1][:], ALU.subtract).then_inc(done, 1)
                dve.wait_ge(done, 4)
                nc.vector.tensor_copy(part[2][:], rest[1][:]).then_inc(done, 1)

            dve.wait_ge(wb_set, 5)
            split(wb, wb_part, wb_rest, wb_split)
            dve.wait_ge(x_loaded, 32)
            split(xs, x_part, x_rest, x_split)
            dve.wait_ge(wb_split, 5)
            dve.wait_ge(const_set, 1)
            for slot, part in enumerate(W_PARTS):
                nc.vector.tensor_copy(w_terms[:, :, slot * PATCH:(slot + 1) * PATCH], wb_part[part][:, :, 0:PATCH])
            for part in range(3):
                last = nc.vector.tensor_copy(w_terms[:, :, BIAS + part], wb_part[part][:, :, PATCH])
            last.then_inc(w_placed, 1)
            dve.wait_ge(ident_loaded, 16)
            nc.vector.tensor_copy(ident16[:], ident[:]).then_inc(w_placed, 1)

            dve.wait_ge(att_loaded, 80)
            nc.vector.tensor_copy(wrep[:].rearrange("p i (r d) -> p i r d", d=HD),
                                  wqk[:].unsqueeze(2).to_broadcast([HD, 3, P // HD, HD])).then_inc(reps_set, 1)
            nc.vector.tensor_copy(erep[:].rearrange("p (r d) -> p r d", d=HD),
                                  ident[0:HD, 0:HD].unsqueeze(1).to_broadcast([HD, P // HD, HD])).then_inc(reps_set, 1)
            dve.wait_ge(w_turned, 1)
            nc.vector.tensor_copy(w_termsT[:, 0:HID], bank16[0][:, 0:HID]).then_inc(w_copied, 1)
            dve.wait_ge(w_turned, 2)
            nc.vector.tensor_copy(wr_termsT[:].rearrange("f (p c) -> f c p", c=HALF),
                                  bank16[1][:, 0:D].rearrange("f (c p) -> f c p", c=HALF)).then_inc(w_copied, 1)
            dve.wait_ge(small_done, 1)
            nc.vector.scalar_tensor_tensor(score_w[:], bank[0][:, 0:P], float(D) ** -0.5, blocks[:],
                                           ALU.mult, ALU.mult).then_inc(small_copied, 1)
            dve.wait_ge(small_done, 2)
            nc.vector.tensor_tensor(wv_blocks[:], bank[1][:, 0:P], blocks[:], ALU.mult).then_inc(small_copied, 1)

            dve.wait_ge(freq_loaded, 64)
            nc.vector.tensor_tensor(rows[:, 0, :], fr[:, 0, :], fr[:, 1, :], ALU.add).then_inc(rows_set, 1)
            nc.vector.tensor_tensor(rows[:, 1, :], fi[:, 0, :], fi[:, 1, :], ALU.subtract).then_inc(rows_set, 1)
            nc.vector.tensor_tensor(rows[:, 2, :], fi[:, 0, :], fi[:, 1, :], ALU.add).then_inc(rows_set, 1)
            nc.vector.tensor_tensor(rows[:, 3, :], fr[:, 1, :], fr[:, 0, :], ALU.subtract).then_inc(rows_set, 1)
            dve.wait_ge(rows_set, 4)
            nc.vector.tensor_copy(rows[0:1, 0, :], fr[0:1, 0, :]).then_inc(rows_set, 1)
            nc.vector.tensor_copy(rows[0:1, 1, :], fr[0:1, 1, :]).then_inc(rows_set, 1)
            nc.vector.tensor_copy(rows[0:1, 2, :], fi[0:1, 0, :]).then_inc(rows_set, 1)
            nc.vector.tensor_copy(rows[0:1, 3, :], fi[0:1, 1, :]).then_inc(rows_set, 1)
            dve.wait_ge(rows_set, 8)
            for i in range(2):
                nc.vector.tensor_tensor(cols[:, i, 1:P], rows[:, i, 1:P], rows[:, i, P + 1:D], ALU.add)
                nc.vector.tensor_copy(cols[:, i, 0:1], rows[:, i, 0:1]).then_inc(cols_set, 1)
            for i in range(2):
                nc.vector.tensor_tensor(cols[:, 2 + i, 1:P], rows[:, 2 + i, P + 1:D], rows[:, 2 + i, 1:P],
                                        ALU.subtract)
                nc.vector.tensor_copy(cols[:, 2 + i, 0:1], rows[:, i, P:P + 1]).then_inc(cols_set, 1)

            def statistics(half):
                with dve.Fori(T // 2 * half, T // 2 * (half + 1)) as t:
                    dve.wait_ge(h_copied, t + 1)
                    nc.vector.bn_stats(tile_of(stats1, t), tile_of(h_all, t)).then_inc(stats1_done, 1)
                tiles = slice(T // 2 * half, T // 2 * (half + 1))
                dve.wait_ge(stats1_done, T // 2 * (half + 1))
                for t in range(T // 2 * half, T // 2 * (half + 1)):
                    nc.vector.bn_aggr(mv1[:, t, :], stats1[:, t, :]).then_inc(mv1_done, 1)
                dve.wait_ge(mv1_done, T // 2 * (half + 1))
                nc.vector.tensor_scalar(ve1[:, tiles], mv1[:, tiles, 1], EPS, None, ALU.add).then_inc(ve1_done, 1)
                dve.wait_ge(rstd1_done, half + 1)
                nc.vector.scalar_tensor_tensor(shift1[:, tiles], mv1[:, tiles, 0], -1.0, rstd1[:, tiles],
                                               ALU.mult, ALU.mult).then_inc(shift1_done, 1)

            statistics(0)
            statistics(1)

            def place_crossed(t, par):
                dve.wait_ge(xh_set, t + 1)
                for b in range(2):
                    e = 1 - b
                    last = nc.vector.tensor_copy(
                        xblk[par][TOK * e:TOK * e + TOK, b, :].rearrange("p (g e d) -> p g e d", e=2, d=HD)[:, :, e, :],
                        xh[par][TOK * b:TOK * b + TOK, :].rearrange("p (g e d) -> p g e d", e=2, d=HD)[:, :, e, :])
                last.then_inc(xblk_crossed, 1)

            def maximum(t, j):
                dve.wait_ge(scores_done, QUADS * t + j + 1)
                nc.vector.tensor_reduce(rowmax[:, j, :], bank[j][:, 0:D].rearrange("p (h k) -> p h k", k=TOK),
                                        AX_X, ALU.max).then_inc(max_done, 1)

            def shift(t, j):
                dve.wait_ge(max_done, QUADS * t + j + 1)
                nc.vector.tensor_tensor(probs[:, j, :].rearrange("p (h k) -> p h k", k=TOK),
                                        bank[j][:, 0:D].rearrange("p (h k) -> p h k", k=TOK),
                                        rowmax[:, j, :].unsqueeze(2).to_broadcast([P, 4, TOK]),
                                        ALU.subtract).then_inc(shifted, 1)


            def divide(t):
                dve.wait_ge(side_copied, t + 1)
                dve.wait_ge(pv_done, t + 1)
                nc.vector.tensor_tensor(onT[:].rearrange("p a t -> p (a t)"), bank[PV_BANK][:, 0:D],
                                        sideT[:, D:2 * D], ALU.mult).then_inc(on_set, 1)

            def finish(t, par):
                dve.wait_ge(h2b_done, t + 1)
                if not first(t, 2):
                    dve.wait_ge(y_stored[par], 16 * (t // 2) if isinstance(t, int) else (t - par) * 8)
                dve.wait_ge(freq_done, t + 1)
                nc.vector.tensor_tensor(y[par][:], bank[SIDE_BANK][:, 0:D], h2b[par][:], ALU.add).then_inc(y_set, 1)

            def residual(t):
                if not first(t, 1):
                    dve.wait_ge(h2b_done, t)
                dve.wait_ge(proj_done, t + 1)
                nc.vector.tensor_tensor(h2[:], bank[PROJ_BANK][:, 0:D], tile_of(hb_all, t), ALU.add).then_inc(h2_done, 1)
                dve.wait_ge(h2_done, t + 1)
                nc.vector.bn_stats(stats2[:], h2[:]).then_inc(stats2_done, 1)
                dve.wait_ge(stats2_done, t + 1)

            def variance(t):
                nc.vector.bn_aggr(mv2[:], stats2[:]).then_inc(mv2_done, 1)
                dve.wait_ge(mv2_done, t + 1)
                nc.vector.tensor_scalar(ve2[:], mv2[:, 1:2], EPS, None, ALU.add).then_inc(ve2_done, 1)

            def inverse_sums(t):
                dve.wait_ge(half_sums_done, 2 * t + 2)
                nc.vector.tensor_reduce(sums[:].rearrange("p q a e -> p (q a e)"),
                                        half_sums[:].rearrange("p q h k -> p (q h) k"), AX_X,
                                        ALU.add).then_inc(sums_done, 1)
                dve.wait_ge(sums_done, t + 1)
                nc.vector.reciprocal(inv_sum[:], sums[:]).then_inc(inv_done, 1)

            def norm2(t):
                dve.wait_ge(rstd2_done, t + 1)
                nc.vector.tensor_scalar(xh2[:], h2[:], mv2[:, 0:1], rstd2[:, 0:1],
                                        ALU.subtract, ALU.mult).then_inc(xh2_set, 1)

            def step(i, par):
                if has(i - 1):
                    finish(i - 1, 1 - par)
                if has(i):
                    residual(i)
                if has(i + 2):
                    place_crossed(i + 2, par)
                if has(i):
                    variance(i)
                if has(i + 1):
                    inverse_sums(i + 1)
                if has(i):
                    norm2(i)
                if has(i + 2):
                    maximum(i + 2, 0)
                if has(i + 2):
                    maximum(i + 2, 1)
                    shift(i + 2, 0)
                    maximum(i + 2, 2)
                    shift(i + 2, 1)
                    maximum(i + 2, 3)
                    shift(i + 2, 2)
                if has(i + 1):
                    divide(i + 1)
                if has(i + 2):
                    shift(i + 2, 3)

            dve.wait_ge(const_set, 6)
            dve.wait_ge(hb_done, T // GROUP)
            for i in range(-2, 2):
                step(i, i % 2)
            with dve.Fori(1, T // 2 - 1) as u:
                step(2 * u, 0)
                step(2 * u + 1, 1)
            for i in range(T - 2, T + 1):
                step(i, i % 2)

        @block.tensor
        def _(pe):
            pe.wait_ge(w_placed, 2)
            for c in range(NC):
                last = pe.transpose(bank16[0][:, c * P:(c + 1) * P], w_terms[:, c, :], ident16[:])
            last.then_inc(w_turned, 1)
            for c in range(HALF):
                last = pe.transpose(bank16[1][:, c * P:(c + 1) * P], w_terms[:, NC + c, :], ident16[:])
            last.then_inc(w_turned, 1)
            pe.wait_ge(wo_loaded, 16)
            for c in range(NC):
                for k in range(HALF):
                    last = pe.transpose(bank[2 + c][:, k * P:(k + 1) * P], wo_raw[:, k, bass.ds(c, P, step=NC)],
                                        ident[:])
                last.then_inc(wo_turned, 1)
            pe.wait_ge(x_placed, 3)
            for t in range(T):
                last = pe.transpose(bank16[6 + t // 8][:, t % 8 * P:(t % 8 + 1) * P], x_terms[:, t, :], ident16[:])
                if t % 8 == 7:
                    last.then_inc(x_turned, 1)
            pe.wait_ge(reps_set, 2)
            pe.wait_ge(w_copied, 2)
            pe.matmul(bank[0][:, 0:P], wrep[:, 0, :], wrep[:, 1, :], start=True, stop=True).then_inc(small_done, 1)
            pe.matmul(bank[1][:, 0:P], erep[:], wrep[:, 2, :], start=True, stop=True).then_inc(small_done, 1)
            pe.wait_ge(small_copied, 2)
            pe.wait_ge(wo_copied, NC)
            pe.wait_ge(x_copied, 2)

            def hidden(t, par):
                if not first(t, 2):
                    pe.wait_ge(silu_done, t - 1)
                for c in range(NC):
                    last = pe.matmul(bank[HID_BANK[par]][:, c * P:(c + 1) * P], w_termsT[:, c * P:(c + 1) * P],
                                     x_termsT[:, bass.ds(t * P, P)], start=True, stop=True)
                last.then_inc(hid_done, 1)

            def mix(t, par):
                pe.wait_ge(silu_done, t + 1)
                if not first(t, 2):
                    pe.wait_ge(h_copied, t - 1)
                for c in range(NC):
                    pe.matmul(bank[MIX_BANK[par]][:, 0:D], hidT[:, par, c * P:(c + 1) * P], woT[:, c, :],
                              start=(c == 0), stop=False)
                pe.matmul(bank[MIX_BANK[par]][:, 0:D], x_termsT[:, bass.ds(t * P, P)], wr_termsT[:],
                          start=False, stop=True).then_inc(mix_done, 1)

            hidden(0, 0)
            hidden(1, 1)
            mix(0, 0)
            hidden(2, 0)
            mix(1, 1)
            with pe.Fori(1, T // 2 - 1) as u:
                hidden(2 * u + 1, 1)
                mix(2 * u, 0)
                hidden(2 * u + 2, 0)
                mix(2 * u + 1, 1)
            hidden(T - 1, 1)
            mix(T - 2, 0)
            mix(T - 1, 1)

            def scores(t):
                for j in range(QUADS):
                    if not first(t, 1):
                        pe.wait_ge(shifted, QUADS * (t - 1) + j + 1)
                    rows32 = slice(32 * j, 32 * j + 32)
                    for half in range(HALF):
                        for b in range(2):
                            last = pe.matmul(bank[j][TOK * b:TOK * b + TOK, half * P:(half + 1) * P],
                                             qT[rows32, half, TOK * b:TOK * b + TOK],
                                             xzT[rows32, 2 * half + b, :, :].rearrange("p e k -> p (e k)"),
                                             start=True, stop=True)
                    last.then_inc(scores_done, 1)

            def side(i):
                if has(i):
                    pe.wait_ge(p_copied, 2 * i + 1)
                if has(i - 1):
                    pe.wait_ge(xh2_set, i)
                    for half in range(HALF):
                        last = pe.transpose(bank[SIDE_BANK][:, half * P:(half + 1) * P],
                                            xh2[:, half * P:(half + 1) * P], ident[:])
                if has(i):
                    pe.wait_ge(inv_spread, i + 1)
                    for half in range(HALF):
                        last = pe.transpose(bank[SIDE_BANK][:, D + half * P:D + (half + 1) * P],
                                            inv_rows[:, half, :, :].rearrange("p h d -> p (h d)"),
                                            ident[:])
                last.then_inc(side_turned, 1)

            def weigh(t, par):
                pe.wait_ge(xblk_same, t + 1)
                pe.wait_ge(xblk_crossed, t + 1)
                pe.wait_ge(p_copied, 2 * (t + 1))
                for half in range(HALF):
                    for b in range(2):
                        for j in range(QUADS):
                            last = pe.matmul(bank[PV_BANK][32 * j:32 * j + 32, half * P + TOK * b:half * P + TOK * (b + 1)],
                                             xblk[par][:, b, half * P + 32 * j:half * P + 32 * j + 32],
                                             pT[:, 2 * j + half, TOK * b:TOK * b + TOK], start=True, stop=True)
                last.then_inc(pv_done, 1)

            def mix_freq(t):
                pe.wait_ge(side_copied, t + 2)
                for half in range(HALF):
                    last = pe.matmul(bank[SIDE_BANK][:, 0:D], sideT[:, half * P:(half + 1) * P], mix_w[:, half, :],
                                     start=(half == 0), stop=(half == HALF - 1))
                last.then_inc(freq_done, 1)

            def project(t):
                pe.wait_ge(on_set, t + 1)
                if not first(t, 1):
                    pe.wait_ge(h2_done, t)
                for half in range(HALF):
                    last = pe.matmul(bank[PROJ_BANK][:, 0:D], onT[:, half, :], value_w[:, half, :],
                                     start=(half == 0), stop=(half == HALF - 1))
                last.then_inc(proj_done, 1)

            def turn_x(t, par):
                pe.wait_ge(xh_set, t + 1)
                if not first(t, 2):
                    pe.wait_ge(p_copied, 2 * (t - 1))
                for half in range(HALF):
                    last = pe.transpose(bank[T1_BANK][:, half * P:(half + 1) * P], xh[par][:, half * P:(half + 1) * P],
                                        ident[:])
                last.then_inc(x1_turned, 1)

            def turn_p(t, part):
                pe.wait_ge(exp_done, QUADS * t + 2 * part + 2)
                if part == 0 and not first(t, 2):
                    pe.wait_ge(y_set, t - 1)
                if part == 1 and has(t + 1):
                    pe.wait_ge(xzT_copied, 2 * (t + 2))
                for k in range(4):
                    j, half = 2 * part + k // 2, k % 2
                    last = pe.transpose(bank[(SIDE_BANK, T1_BANK)[part]][:, k * P:(k + 1) * P],
                                        probs[:, j, half * P:(half + 1) * P], ident[:])
                last.then_inc(p_turned, 1)

            def query(t):
                pe.wait_ge(xT_copied, t + 1)
                if not first(t, 2):
                    pe.wait_ge(on_set, t - 1)
                for half in range(HALF):
                    last = pe.matmul(bank[PV_BANK][:, half * P:(half + 1) * P], score_w[:],
                                     xT[:, half * P:(half + 1) * P], start=True, stop=True)
                last.then_inc(q_done, 1)

            def step(i, par):
                if has(i + 1):
                    pe.wait_ge(xzT_copied, 2 * (i + 2))
                    pe.wait_ge(q_copied, i + 2)
                    scores(i + 1)
                if has(i) or has(i - 1):
                    side(i)
                if has(i):
                    weigh(i, par)
                if has(i + 2):
                    turn_x(i + 2, par)
                if has(i - 1):
                    mix_freq(i - 1)
                if has(i):
                    project(i)
                if has(i + 2):
                    query(i + 2)
                if has(i + 1):
                    turn_p(i + 1, 0)
                    turn_p(i + 1, 1)

            pe.wait_ge(wout_loaded, 16)
            pe.wait_ge(silu_done, T)
            for c in range(HALF):
                for k in range(HALF):
                    last = pe.transpose(bank[c][:, k * P:(k + 1) * P], wout_raw[:, k, c * P:(c + 1) * P], ident[:])
                last.then_inc(wout_turned, 1)
            pe.wait_ge(cols_set, 4)
            for c in range(2):
                pe.matmul(bank[2 + c][:, 0:D], cols[:, 2 * c, :], cosine[:], start=True, stop=False)
                pe.matmul(bank[2 + c][:, 0:D], cols[:, 2 * c + 1, :], sine[:], start=False,
                          stop=True).then_inc(halfway_done, 1)
            turn_x(0, 0)
            pe.wait_ge(wout_copied, HALF)
            for c in range(HALF):
                pe.matmul(bank[c][:, 0:D], wv_blocks[:], woutT[:, c, :], start=True, stop=True).then_inc(value_done, 1)
            query(0)
            pe.wait_ge(halfway_copied, 2)
            for c in range(HALF):
                pe.matmul(bank[2 + c][:, 0:D], halfway[:, 0, c * P:(c + 1) * P], cosine[:], start=True, stop=False)
                pe.matmul(bank[2 + c][:, 0:D], halfway[:, 1, c * P:(c + 1) * P], sine[:], start=False,
                          stop=True).then_inc(mixw_done, 1)
            pe.wait_ge(value_copied, HALF)
            pe.wait_ge(mixw_copied, HALF)
            for i in range(-1, 2):
                step(i, i % 2)
            with pe.Fori(1, T // 2 - 1) as u:
                step(2 * u, 0)
                step(2 * u + 1, 1)
            for i in range(T - 2, T + 1):
                step(i, i % 2)


_INS = {
    "x": "x", "L0_tok_W_h": "W_h", "L0_tok_b_h": "b_h", "L0_tok_W_o": "W_o", "L0_tok_b_o": "b_o",
    "L0_tok_W_r": "W_r", "L0_tok_b_r": "b_r", "L0_attn_Wq": "Wq", "L0_attn_Wk": "Wk", "L0_attn_Wv": "Wv",
    "L0_attn_W_out": "W_out", "L0_attn_b_out": "b_out", "L0_ffn_w_freq_real": "wr", "L0_ffn_w_freq_imag": "wi",
    "L0_ffn_bias": "bias",
}


def kernel(**inputs):
    import concourse.bacc as _bacc
    from concourse.bass_utils import run_bass_kernel_spmd as _run

    nc = _bacc.Bacc("TRN2", target_bir_lowering=False, num_devices=1)
    arrays, args = {}, {}
    data = {short: np.asarray(inputs[name]) for name, short in _INS.items()}
    for short in ("wr", "wi"):
        data[short] = data[short][FOLDED][:, FOLDED]
    data.update(launch_constants())
    for short, v in data.items():
        v = np.ascontiguousarray(v)
        arrays[f"in_{short}"] = v
        args[short] = nc.dram_tensor(f"in_{short}", v.shape, mybir.dt.from_np(v.dtype), kind="ExternalInput").ap()
    out = nc.dram_tensor("out_0", (BATCH, TOK, D), F32, kind="ExternalOutput").ap()
    audio_tower_kernel(nc, args, out)
    r = _run(nc, [arrays], core_ids=[0])
    return r.results[0]["out_0"]
```

```python
from contextlib import ExitStack

import concourse.bass as bass
import numpy as np
from concourse import mybir

F32 = mybir.dt.float32
BF16 = mybir.dt.bfloat16
F32R = mybir.dt.float32r
ALU = mybir.AluOpType
ACT = mybir.ActivationFunctionType
AX_X = mybir.AxisListType.X

P = 128
BATCH, LENGTH = 32, 1024
PATCH = 16
TOK = LENGTH // PATCH
TERMS = 6
TERM = PATCH + 1
STACK = TERMS * TERM
HID = 512
NC = HID // P
D = 256
HEADS, HD = 16, 16
T = BATCH * TOK // P
GROUP = 4
HALF = D // P
QUADS = 4
EPS = 1e-5


def launch_constants():
    k = np.arange(P)[:, None].astype(np.float64)
    n = np.arange(D)[None, :].astype(np.float64)
    cosine = np.cos(2 * np.pi * k * n / D)
    sine = np.sin(2 * np.pi * k * n / D)
    sine[0] = np.cos(np.pi * n[0])
    r = np.arange(P)
    head_blocks = (r[:, None] // HD == r[None, :] // HD).astype(np.float32)
    parity = (np.stack([r // HD % 2, r // HD % 2, r // TOK, r // TOK], 1) == [0, 1, 0, 1]).astype(np.float32)
    return {
        "identity": np.eye(P, dtype=np.float32),
        "head_blocks": head_blocks,
        "parity": parity,
        "cosine": cosine.astype(np.float32),
        "sine": sine.astype(np.float32),
    }


FOLDED = np.concatenate([np.arange(P), [P], np.arange(D - 1, P, -1)])


def audio_tower_kernel(nc, a, out):
    with ExitStack() as ctx:
        def sb(name, shape, dtype=F32):
            return ctx.enter_context(nc.sbuf_tensor(name, shape, dtype))

        def sem(name):
            return ctx.enter_context(nc.semaphore(name))

        ident = sb("ident", [P, P])
        ident16 = sb("ident16", [P, P], BF16)
        blocks = sb("blocks", [P, P])
        parity = sb("parity_sb", [P, 4])
        cosine = sb("cosine_sb", [P, D])
        sine = sb("sine_sb", [P, D])
        bh = sb("bh", [P, NC])
        br = sb("br", [P, HALF])
        bo = sb("bo", [P, HALF])
        wf_raw = sb("wf_raw", [P, NC + HALF, 2 * PATCH])
        wb = sb("wb", [P, NC + HALF, TERM])
        wb_rest = [sb(f"wb_rest{i}", [P, NC + HALF, TERM]) for i in range(2)]
        w_terms = sb("w_terms", [P, NC + HALF, P], BF16)
        w_termsT = sb("w_termsT", [P, (NC + HALF) * P], BF16)
        wr_termsT = sb("wr_termsT", [P, D], BF16)
        wo_raw = sb("wo_raw", [P, HALF, HID])
        wout_raw = sb("wout_raw", [P, HALF, D])
        wo_hi = sb("wo_hi", [P, NC, D], F32R)
        wo_lo = sb("wo_lo", [P, NC, D], F32R)
        woutT = sb("woutT", [P, HALF, D])
        wqk = sb("wqk", [HD, 3, HD])
        wrep = sb("wrep", [HD, 3, P])
        erep = sb("erep", [HD, P])
        score_w = sb("score_w", [P, P])
        wv_blocks = sb("wv_blocks", [P, P])
        value_w = sb("value_w", [P, HALF, D])
        fr = sb("fr", [P, 2, D])
        fi = sb("fi", [P, 2, D])
        rows = sb("rows", [P, 4, D])
        cols = sb("cols", [P, 4, P])
        halfway = sb("halfway", [P, 2, D])
        mix_w = sb("mix_w", [P, HALF, D])
        bout_bc = sb("bout_bc", [P, D])
        fbias_bc = sb("fbias_bc", [P, D])
        xs = sb("xs", [P, T, PATCH])
        x_rest = [sb(f"x_rest{i}", [P, T, PATCH]) for i in range(2)]
        x_terms = sb("x_terms", [P, T, P], BF16)
        x_termsT = sb("x_termsT", [P, T * P], BF16)
        hidT = sb("hidT", [P, 2, HID])
        hid_hi = sb("hid_hi", [P, 2, HID], F32R)
        hid_lo = sb("hid_lo", [P, 2, HID], F32R)
        h_all = sb("h_all", [P, T, D])
        hb_all = sb("hb_all", [P, T, D])
        stats1 = sb("stats1", [P, T, 6])
        mv1 = sb("mv1", [P, T, 2])
        ve1 = sb("ve1", [P, T])
        rstd1 = sb("rstd1", [P, T])
        shift1 = sb("shift1", [P, T])
        half_neg = sb("half_neg", [P, T])
        warm = sb("warm", [P, 1])
        xh = [sb(f"xh{i}", [P, D]) for i in range(2)]
        xblk = [sb(f"xblk{i}", [P, 2, D]) for i in range(2)]
        xT = sb("xT", [P, D])
        xzT = sb("xzT", [P, 2 * HALF, 2, TOK])
        qT = sb("qT", [P, HALF, P])
        rowmax = sb("rowmax", [P, QUADS, 4])
        probs = sb("probs", [P, QUADS, D])
        half_sums = sb("half_sums", [P, QUADS, 4, TOK // 2])
        sums = sb("sums", [P, QUADS, HALF, 2])
        inv_sum = sb("inv_sum", [P, QUADS, HALF, 2])
        inv_rows = sb("inv_rows", [P, HALF, 2 * QUADS, HD])
        pT = sb("pT", [P, 2 * QUADS, P])
        sideT = sb("sideT", [P, 2 * D])
        onT = sb("onT", [P, HALF, P])
        h2 = sb("h2", [P, D])
        h2b = [sb(f"h2b{i}", [P, D]) for i in range(2)]
        stats2 = sb("stats2", [P, 6])
        mv2 = sb("mv2", [P, 2])
        ve2 = sb("ve2", [P, 1])
        rstd2 = sb("rstd2", [P, 1])
        xh2 = sb("xh2", [P, D])
        y = [sb(f"y{i}", [P, D]) for i in range(2)]

        bank = [ctx.enter_context(nc.psum_tensor(f"bank{i}", [P, 512], F32)) for i in range(8)]
        bank16 = [b[:].bitcast(BF16) for b in bank]
        HID_BANK, MIX_BANK = (0, 1), (5, 6)
        WO_BANK = (2, 3, 4, 6)
        HALFWAY_BANK = (3, 6)
        T1_BANK, SIDE_BANK, PROJ_BANK, PV_BANK = 4, 5, 6, 7

        b_loaded = sem("b_loaded")
        x_loaded, w_loaded, wo_loaded = sem("x_loaded"), sem("w_loaded"), sem("wo_loaded")
        ident_loaded, att_loaded, wout_loaded, freq_loaded, bias_loaded = (
            sem("ident_loaded"), sem("att_loaded"), sem("wout_loaded"), sem("freq_loaded"), sem("bias_loaded"))
        const_set, wb_set, ident16_set = sem("const_set"), sem("wb_set"), sem("ident16_set")
        w_placed, w_rest_set, x_placed, x_rest_set = (
            sem("w_placed"), sem("w_rest_set"), sem("x_placed"), sem("x_rest_set"))
        x_late_copied = sem("x_late_copied")
        w_turned, w_copied, x_turned, x_copied = sem("w_turned"), sem("w_copied"), sem("x_turned"), sem("x_copied")
        wo_turned, wo_copied = sem("wo_turned"), sem("wo_copied")
        reps_set, small_done, small_copied = sem("reps_set"), sem("small_done"), sem("small_copied")
        wout_turned, wout_copied, value_done, value_copied = (
            sem("wout_turned"), sem("wout_copied"), sem("value_done"), sem("value_copied"))
        rows_set, cols_set = sem("rows_set"), sem("cols_set")
        halfway_done, halfway_copied, mixw_done, mixw_copied = (
            sem("halfway_done"), sem("halfway_copied"), sem("mixw_done"), sem("mixw_copied"))
        hi_done, lo_done, wo_split = sem("hi_done"), sem("lo_done"), sem("wo_split")
        hid_done, silu_done, mix_done = sem("hid_done"), sem("silu_done"), sem("mix_done")
        h_copied, hb_done, stats1_done, mv1_done, ve1_done, rstd1_done, shift1_done = (
            sem("h_copied"), sem("hb_done"), sem("stats1_done"), sem("mv1_done"), sem("ve1_done"),
            sem("rstd1_done"), sem("shift1_done"))
        xh_set, x1_turned, xT_copied, xzT_copied = sem("xh_set"), sem("x1_turned"), sem("xT_copied"), sem("xzT_copied")
        xblk_same, xblk_crossed = sem("xblk_same"), sem("xblk_crossed")
        q_done, q_copied = sem("q_done"), sem("q_copied")
        scores_done, max_done, shifted, exp_done = sem("scores_done"), sem("max_done"), sem("shifted"), sem("exp_done")
        half_sums_done, sums_done, inv_done, inv_spread = (
            sem("half_sums_done"), sem("sums_done"), sem("inv_done"), sem("inv_spread"))
        side_turned, side_copied = sem("side_turned"), sem("side_copied")
        p_turned, p_copied, pv_done, on_set = sem("p_turned"), sem("p_copied"), sem("pv_done"), sem("on_set")
        proj_done, h2_done = sem("proj_done"), sem("h2_done")
        stats2_done, mv2_done, ve2_done, rstd2_done = sem("stats2_done"), sem("mv2_done"), sem("ve2_done"), sem("rstd2_done")
        h2b_done, xh2_set, freq_done, y_set = sem("h2b_done"), sem("xh2_set"), sem("freq_done"), sem("y_set")
        y_stored = [sem("y_stored0"), sem("y_stored1")]

        x_tok = a["x"].rearrange("b (n f) -> (b n) f", f=PATCH).rearrange("(t p) f -> p t f", p=P)
        out_tok = out.rearrange("b n d -> (b n) d").rearrange("(t p) d -> p t d", p=P)

        def tile_of(tensor, t):
            return tensor[:, bass.ds(t, 1), :].rearrange("p o n -> p (o n)")

        def first(t, n):
            return isinstance(t, int) and t < n

        def at(i, n):
            return isinstance(i, int) and i == n

        def has(t):
            return not isinstance(t, int) or 0 <= t < T

        X_SLOTS = (slice(0, 3), slice(3, 5), slice(5, 6))
        W_SLOTS = (slice(1, 6, 2), slice(2, 5, 2), slice(0, 1))
        x_slots = x_terms[:, :, 0:STACK].rearrange("p t (n f) -> p t n f", f=TERM)
        w_slots = w_terms[:, :, 0:STACK].rearrange("p c (n f) -> p c n f", f=TERM)

        block = ctx.enter_context(nc.Block())

        @block.sync
        def _(sp):
            sp.dma_start(xs[:], x_tok).then_inc(x_loaded, 16)
            sp.dma_start(bh[:], a["b_h"].rearrange("(p c) -> p c", p=P)).then_inc(b_loaded, 16)
            sp.dma_start(br[:], a["b_r"].rearrange("(p c) -> p c", p=P)).then_inc(b_loaded, 16)
            sp.dma_start(bo[:], a["b_o"].rearrange("(p c) -> p c", p=P)).then_inc(b_loaded, 16)
            sp.dma_start(ident[:], a["identity"]).then_inc(ident_loaded, 16)
            sp.dma_start(wo_raw[:], a["W_o"].rearrange("(c p) i -> p c i", p=P)).then_inc(wo_loaded, 16)
            for i, name in enumerate(("Wq", "Wk", "Wv")):
                sp.dma_start(wqk[:, i, :], a[name]).then_inc(att_loaded, 16)
            sp.dma_start(blocks[:], a["head_blocks"]).then_inc(att_loaded, 16)
            sp.dma_start(parity[:], a["parity"]).then_inc(att_loaded, 16)
            sp.dma_start(wout_raw[:], a["W_out"].rearrange("(c p) i -> p c i", p=P)).then_inc(wout_loaded, 16)
            sp.dma_start(bout_bc[:], a["b_out"].partition_broadcast(P)).then_inc(bias_loaded, 16)
            for name, dst in (("wr", fr), ("wi", fi)):
                sp.dma_start(dst[:], a[name].rearrange("(c p) n -> p c n", p=P)).then_inc(freq_loaded, 16)
            sp.dma_start(cosine[:], a["cosine"]).then_inc(freq_loaded, 16)
            sp.dma_start(sine[:], a["sine"]).then_inc(freq_loaded, 16)
            sp.dma_start(fbias_bc[:], a["bias"].partition_broadcast(P)).then_inc(bias_loaded, 16)

            def store(t, par):
                sp.wait_ge(y_set, t + 1)
                sp.dma_start(tile_of(out_tok, t), y[par][:]).then_inc(y_stored[par], 16)

            with sp.Fori(0, T // 2) as u:
                store(2 * u, 0)
                store(2 * u + 1, 1)
            for par in range(2):
                sp.wait_ge(y_stored[par], 16 * (T // 2))

        @block.scalar
        def _(act):
            act.dma_start(wf_raw[:, 0:NC, :], a["W_h"].rearrange("(p c) f -> p c f", p=P)).then_inc(w_loaded, 16)
            act.dma_start(wf_raw[:, NC:, :], a["W_r"].rearrange("(p c) f -> p c f", p=P)).then_inc(w_loaded, 16)

            act.wait_ge(const_set, 1)
            nc.scalar.activation(warm[:], half_neg[:, 0:1], ACT.Silu)
            act.wait_ge(x_loaded, 16)
            for part, src in enumerate((xs, *x_rest)):
                n = X_SLOTS[part].stop - X_SLOTS[part].start
                if part > 0:
                    act.wait_ge(x_rest_set, part)
                nc.scalar.activation(x_slots[:, :, X_SLOTS[part], 0:PATCH],
                                     src[:].unsqueeze(2).to_broadcast([P, T, n, PATCH]), ACT.Copy).then_inc(x_placed, 1)
            for g in range(2):
                act.wait_ge(x_turned, g + 1)
                nc.scalar.activation(x_termsT[:, g * HID:(g + 1) * HID], bank16[6 + g][:, 0:HID],
                                     ACT.Copy).then_inc(x_copied, 1)

            def wo_leading(chunks):
                for c in chunks:
                    act.wait_ge(wo_turned, c + 1)
                    nc.scalar.activation(wo_hi[:, c, :], bank[WO_BANK[c]][:, 0:D], ACT.Copy).then_inc(wo_copied, 1)

            def silu(t, par):
                act.wait_ge(hid_done, t + 1)
                if not first(t, 2):
                    act.wait_ge(mix_done, t - 1)
                nc.scalar.activation(hid_hi[:, par, :], bank[HID_BANK[par]][:], ACT.Silu).then_inc(hi_done, 1)
                if at(t, 0):
                    wo_leading((2, 3))
                nc.scalar.activation(hidT[:, par, :], bank[HID_BANK[par]][:], ACT.Silu).then_inc(silu_done, 1)

            def copy_h(t, par):
                act.wait_ge(mix_done, t + 1)
                nc.scalar.activation(tile_of(h_all, t), bank[MIX_BANK[par]][:, 0:D], ACT.Copy).then_inc(h_copied, 1)

            wo_leading((0, 1))
            silu(0, 0)
            silu(1, 1)
            copy_h(0, 0)
            silu(2, 0)
            copy_h(1, 1)
            with act.Fori(1, T // 2 - 1) as u:
                silu(2 * u + 1, 1)
                copy_h(2 * u, 0)
                silu(2 * u + 2, 0)
                copy_h(2 * u + 1, 1)

            def normalize(t, par):
                act.wait_ge(shift1_done, (t // (T // 2) + 1) if isinstance(t, int) else 2)
                if not first(t, 2):
                    act.wait_ge(xblk_same, t - 1)
                    act.wait_ge(xblk_crossed, t - 1)
                nc.scalar.activation(xh[par][:], tile_of(h_all, t), ACT.Identity,
                                     bias=shift1[:, bass.ds(t, 1)], scale=rstd1[:, bass.ds(t, 1)]).then_inc(xh_set, 1)

            def spread_inverse(t):
                act.wait_ge(inv_done, t + 1)
                for half in range(HALF):
                    last = nc.scalar.activation(
                        inv_rows[:, half, :, :].rearrange("p (q e) d -> p q e d", e=2),
                        inv_sum[:, :, half, :].unsqueeze(3).to_broadcast([P, QUADS, 2, HD]), ACT.Copy)
                last.then_inc(inv_spread, 1)

            def exponent(t, j):
                act.wait_ge(shifted, QUADS * t + j + 1)
                nc.scalar.activation(probs[:, j, :], probs[:, j, :], ACT.Exp).then_inc(exp_done, 1)

            def copy_side(lo, hi, n):
                act.wait_ge(side_turned, n)
                nc.scalar.activation(sideT[:, lo:hi], bank[SIDE_BANK][:, lo:hi], ACT.Copy).then_inc(side_copied, 1)

            def copy_xT(t):
                act.wait_ge(x1_turned, t + 1)
                nc.scalar.activation(xT[:], bank[T1_BANK][:, 0:D], ACT.Copy).then_inc(xT_copied, 1)

            def copy_xzT(t):
                act.wait_ge(x1_turned, t + 1)
                for e in range(2):
                    nc.scalar.activation(xzT[:, :, e, :], bank[T1_BANK][:, 0:D].rearrange("p (g k) -> p g k", k=TOK),
                                         ACT.Copy, scale=parity[:, e:e + 1]).then_inc(xzT_copied, 1)

            def copy_q(t):
                act.wait_ge(q_done, t + 1)
                nc.scalar.activation(qT[:].rearrange("p a t -> p (a t)"), bank[PV_BANK][:, 0:D],
                                     ACT.Copy).then_inc(q_copied, 1)

            def copy_p(t, part):
                act.wait_ge(p_turned, 2 * t + part + 1)
                nc.scalar.activation(pT[:, 4 * part:4 * part + 4, :].rearrange("p a t -> p (a t)"),
                                     bank[(SIDE_BANK, T1_BANK)[part]][:], ACT.Copy).then_inc(p_copied, 1)

            def copy_halfway(c):
                act.wait_ge(halfway_done, c + 1)
                nc.scalar.activation(halfway[:, c, :], bank[HALFWAY_BANK[c]][:, 0:D], ACT.Copy).then_inc(halfway_copied, 1)

            def copy_value_weights():
                for c in range(HALF):
                    act.wait_ge(value_done, c + 1)
                    nc.scalar.activation(value_w[:, c, :], bank[2 + c][:, 0:D], ACT.Copy).then_inc(value_copied, 1)

            def copy_mix_weights(c):
                act.wait_ge(mixw_done, c + 1)
                nc.scalar.activation(mix_w[:, c, :], bank[PROJ_BANK][:, 0:D], ACT.Copy, scale=1.0 / D).then_inc(mixw_copied, 1)

            def step(i, par):
                if has(i):
                    spread_inverse(i)
                if has(i + 2):
                    normalize(i + 2, par)
                if at(i, 1):
                    copy_mix_weights(1)
                copy_side(0 if has(i - 1) else D, 2 * D if has(i) else D, i + 1)
                if has(i + 1):
                    exponent(i + 1, 0)
                    exponent(i + 1, 1)
                if has(i + 2):
                    copy_xT(i + 2)
                    copy_xzT(i + 2)
                if has(i + 1):
                    exponent(i + 1, 2)
                    exponent(i + 1, 3)
                if has(i + 2):
                    copy_q(i + 2)
                if has(i + 1):
                    copy_p(i + 1, 0)
                    copy_p(i + 1, 1)

            act.wait_ge(att_loaded, 80)
            normalize(0, 0)
            silu(T - 1, 1)
            copy_halfway(0)
            copy_xT(0)
            copy_xzT(0)
            copy_h(T - 2, 0)
            copy_q(0)
            nc.scalar.activation(warm[:], half_neg[:, 0:1], ACT.Exp)
            copy_h(T - 1, 1)
            normalize(1, 1)
            exponent(0, 0)
            copy_xT(1)
            for j in range(1, QUADS):
                exponent(0, j)
            copy_xzT(1)
            copy_halfway(1)
            copy_q(1)
            copy_p(0, 0)
            copy_p(0, 1)
            copy_value_weights()
            spread_inverse(0)
            normalize(2, 0)
            for j in range(QUADS):
                exponent(1, j)
            copy_side(D, 2 * D, 1)
            copy_mix_weights(0)
            copy_xT(2)
            copy_xzT(2)
            copy_p(1, 0)
            copy_q(2)
            copy_p(1, 1)
            step(1, 1)
            with act.Fori(1, T // 2 - 1) as u:
                step(2 * u, 0)
                step(2 * u + 1, 1)
            for i in range(T - 2, T + 1):
                step(i, i % 2)

        @block.gpsimd
        def _(pool):
            nc.gpsimd.memset(half_neg[:], -0.5).then_inc(const_set, 1)
            nc.gpsimd.memset(w_terms[:, :, STACK:P], 0.0).then_inc(const_set, 1)
            nc.gpsimd.memset(x_terms[:, :, STACK:P], 0.0).then_inc(const_set, 1)
            nc.gpsimd.memset(x_slots[:, :, 0:3, PATCH], 1.0).then_inc(const_set, 1)
            nc.gpsimd.memset(x_slots[:, :, 3:TERMS, PATCH], 0.0).then_inc(const_set, 1)
            for i in range(2):
                nc.gpsimd.memset(xblk[i][:], 0.0).then_inc(const_set, 1)
            pool.wait_ge(ident_loaded, 16)
            nc.gpsimd.tensor_copy(ident16[:], ident[:]).then_inc(ident16_set, 1)

            pool.wait_ge(att_loaded, 80)
            nc.gpsimd.tensor_copy(wrep[:].rearrange("p i (r d) -> p i r d", d=HD),
                                  wqk[:].unsqueeze(2).to_broadcast([HD, 3, P // HD, HD])).then_inc(reps_set, 1)
            nc.gpsimd.tensor_copy(erep[:].rearrange("p (r d) -> p r d", d=HD),
                                  ident[0:HD, 0:HD].unsqueeze(1).to_broadcast([HD, P // HD, HD])).then_inc(reps_set, 1)
            pool.wait_ge(const_set, 7)
            pool.wait_ge(freq_loaded, 64)
            nc.gpsimd.tensor_tensor(rows[:, 0, :], fr[:, 0, :], fr[:, 1, :], ALU.add).then_inc(rows_set, 1)
            nc.gpsimd.tensor_tensor(rows[:, 1, :], fi[:, 0, :], fi[:, 1, :], ALU.subtract).then_inc(rows_set, 1)
            nc.gpsimd.tensor_tensor(rows[:, 2, :], fi[:, 0, :], fi[:, 1, :], ALU.add).then_inc(rows_set, 1)
            nc.gpsimd.tensor_tensor(rows[:, 3, :], fr[:, 1, :], fr[:, 0, :], ALU.subtract).then_inc(rows_set, 1)
            pool.wait_ge(rows_set, 4)
            nc.gpsimd.tensor_copy(rows[0:1, 0, :], fr[0:1, 0, :]).then_inc(rows_set, 1)
            nc.gpsimd.tensor_copy(rows[0:1, 1, :], fr[0:1, 1, :]).then_inc(rows_set, 1)
            nc.gpsimd.tensor_copy(rows[0:1, 2, :], fi[0:1, 0, :]).then_inc(rows_set, 1)
            nc.gpsimd.tensor_copy(rows[0:1, 3, :], fi[0:1, 1, :]).then_inc(rows_set, 1)
            pool.wait_ge(rows_set, 8)
            for i in range(2):
                nc.gpsimd.tensor_tensor(cols[:, i, 1:P], rows[:, i, 1:P], rows[:, i, P + 1:D], ALU.add)
                nc.gpsimd.tensor_copy(cols[:, i, 0:1], rows[:, i, 0:1]).then_inc(cols_set, 1)
            for i in range(2):
                nc.gpsimd.tensor_tensor(cols[:, 2 + i, 1:P], rows[:, 2 + i, P + 1:D], rows[:, 2 + i, 1:P],
                                        ALU.subtract)
                nc.gpsimd.tensor_copy(cols[:, 2 + i, 0:1], rows[:, i, P:P + 1]).then_inc(cols_set, 1)

            pool.wait_ge(bias_loaded, 32)

            def residual_bias(g):
                tiles = slice(GROUP * g, GROUP * (g + 1))
                pool.wait_ge(h_copied, GROUP * (g + 1))
                nc.gpsimd.tensor_tensor(hb_all[:, tiles, :], h_all[:, tiles, :],
                                        bout_bc[:].unsqueeze(1).to_broadcast([P, GROUP, D]),
                                        ALU.add).then_inc(hb_done, 1)

            def inv_std1(half):
                tiles = slice(T // 2 * half, T // 2 * (half + 1))
                pool.wait_ge(ve1_done, half + 1)
                nc.gpsimd.tensor_tensor(rstd1[:, tiles], ve1[:, tiles], half_neg[:, tiles],
                                        ALU.pow).then_inc(rstd1_done, 1)

            residual_bias(0)
            residual_bias(1)
            inv_std1(0)
            residual_bias(2)

            def halve_sums(t, part):
                quads = slice(2 * part, 2 * part + 2)
                pr = probs[:, quads, :].rearrange("p q (h s k) -> p (q h) s k", s=2, k=TOK // 2)
                nc.gpsimd.tensor_tensor(half_sums[:, quads, :, :].rearrange("p q h k -> p (q h) k"),
                                        pr[:, :, 0, :], pr[:, :, 1, :], ALU.add).then_inc(half_sums_done, 1)

            def place_same(par):
                for b in range(2):
                    last = nc.gpsimd.tensor_scalar(
                        xblk[par][:, b, :].rearrange("p (g e d) -> p g e d", e=2, d=HD)[:, :, b, :],
                        xh[par][:].rearrange("p (g e d) -> p g e d", e=2, d=HD)[:, :, b, :],
                        parity[:, 2 + b:3 + b], 1.0, ALU.mult, ALU.mult)
                last.then_inc(xblk_same, 1)

            def inv_std2(t):
                pool.wait_ge(ve2_done, t + 1)
                if not first(t, 1):
                    pool.wait_ge(xh2_set, t)
                nc.gpsimd.tensor_tensor(rstd2[:], ve2[:], half_neg[:, 0:1], ALU.pow).then_inc(rstd2_done, 1)

            def add_bias(t, par):
                if not first(t, 2):
                    pool.wait_ge(y_set, t - 1)
                nc.gpsimd.tensor_tensor(h2b[par][:], h2[:], fbias_bc[:], ALU.add).then_inc(h2b_done, 1)

            def step(i, par):
                if has(i + 1):
                    pool.wait_ge(exp_done, QUADS * (i + 1) + 2)
                    if not first(i + 1, 1):
                        pool.wait_ge(sums_done, i + 1)
                    halve_sums(i + 1, 0)
                    if has(i + 2):
                        pool.wait_ge(xh_set, i + 3)
                        if has(i):
                            pool.wait_ge(pv_done, i + 1)
                    pool.wait_ge(exp_done, QUADS * (i + 1) + 4)
                    halve_sums(i + 1, 1)
                if has(i + 2):
                    place_same(par)
                if has(i):
                    inv_std2(i)
                    add_bias(i, par)

            pool.wait_ge(xh_set, 1)
            place_same(0)
            step(-1, 1)
            step(0, 0)
            inv_std1(1)
            step(1, 1)
            residual_bias(3)
            with pool.Fori(1, T // 2 - 1) as u:
                step(2 * u, 0)
                step(2 * u + 1, 1)
            for i in range(T - 2, T):
                step(i, i % 2)

        @block.vector
        def _(dve):
            def place_w(part, src):
                n = len(range(*W_SLOTS[part].indices(TERMS)))
                nc.vector.tensor_copy(w_slots[:, :, W_SLOTS[part], :],
                                      src[:].unsqueeze(2).to_broadcast([P, NC + HALF, n, TERM])).then_inc(w_placed, 1)

            def w_remainder(part, src):
                dve.wait_ge(w_placed, part + 1)
                nc.vector.tensor_tensor(wb_rest[part][:], src[:], w_slots[:, :, W_SLOTS[part].start, :],
                                        ALU.subtract).then_inc(w_rest_set, 1)

            def x_remainder(part, src):
                dve.wait_ge(x_placed, part + 1)
                nc.vector.tensor_tensor(x_rest[part][:], src[:], x_slots[:, :, X_SLOTS[part].start, 0:PATCH],
                                        ALU.subtract).then_inc(x_rest_set, 1)

            dve.wait_ge(w_loaded, 32)
            nc.vector.tensor_copy(wb[:, :, 0:PATCH], wf_raw[:, :, 0:PATCH]).then_inc(wb_set, 1)
            nc.vector.tensor_reduce(wb[:, :, PATCH], wf_raw[:, :, PATCH:], AX_X, ALU.add).then_inc(wb_set, 1)
            x_remainder(0, xs)
            dve.wait_ge(b_loaded, 48)
            nc.vector.tensor_tensor(br[:], br[:], bo[:], ALU.add).then_inc(wb_set, 1)
            dve.wait_ge(wb_set, 3)
            nc.vector.tensor_tensor(wb[:, 0:NC, PATCH], wb[:, 0:NC, PATCH], bh[:], ALU.add).then_inc(wb_set, 1)
            nc.vector.tensor_tensor(wb[:, NC:, PATCH], wb[:, NC:, PATCH], br[:], ALU.add).then_inc(wb_set, 1)
            dve.wait_ge(wb_set, 5)
            place_w(0, wb)
            w_remainder(0, wb)
            dve.wait_ge(w_rest_set, 1)
            place_w(1, wb_rest[0])
            w_remainder(1, wb_rest[0])
            dve.wait_ge(x_rest_set, 1)
            x_remainder(1, x_rest[0])
            dve.wait_ge(w_rest_set, 2)
            place_w(2, wb_rest[1])

            def wo_remainder(chunks):
                for c in chunks:
                    dve.wait_ge(wo_copied, c + 1)
                    nc.vector.tensor_tensor(wo_lo[:, c, :], bank[WO_BANK[c]][:, 0:D], wo_hi[:, c, :].bitcast(F32),
                                            ALU.subtract).then_inc(wo_split, 1)

            def remainder(t, par):
                dve.wait_ge(silu_done, t + 1)
                nc.vector.tensor_tensor(hid_lo[:, par, :], hidT[:, par, :], hid_hi[:, par, :].bitcast(F32),
                                        ALU.subtract).then_inc(lo_done, 1)

            dve.wait_ge(w_turned, 1)
            nc.vector.tensor_copy(w_termsT[:, 0:HID], bank16[0][:, 0:HID]).then_inc(w_copied, 1)
            dve.wait_ge(w_turned, 2)
            nc.vector.tensor_copy(wr_termsT[:].rearrange("f (p c) -> f c p", c=HALF),
                                  bank16[1][:, 0:D].rearrange("f (c p) -> f c p", c=HALF)).then_inc(w_copied, 1)
            wo_remainder(range(NC))
            remainder(0, 0)
            remainder(1, 1)
            dve.wait_ge(x_turned, 3)
            nc.vector.tensor_copy(x_termsT[:, 2 * HID:], bank16[7]).then_inc(x_late_copied, 1)
            dve.wait_ge(small_done, 2)
            nc.vector.scalar_tensor_tensor(score_w[:], bank[4][:, 0:P], float(D) ** -0.5, blocks[:],
                                           ALU.mult, ALU.mult).then_inc(small_copied, 1)
            nc.vector.tensor_tensor(wv_blocks[:], bank[4][:, P:2 * P], blocks[:], ALU.mult).then_inc(small_copied, 1)
            for c in range(HALF):
                dve.wait_ge(wout_turned, c + 1)
                nc.vector.tensor_copy(woutT[:, c, :], bank[2 + c][:, 0:D]).then_inc(wout_copied, 1)

            def h_stats(t):
                dve.wait_ge(h_copied, t + 1)
                nc.vector.bn_stats(tile_of(stats1, t), tile_of(h_all, t)).then_inc(stats1_done, 1)

            def variance1(half):
                tiles = slice(T // 2 * half, T // 2 * (half + 1))
                dve.wait_ge(stats1_done, T // 2 * (half + 1))
                for t in range(T // 2 * half, T // 2 * (half + 1)):
                    nc.vector.bn_aggr(mv1[:, t, :], stats1[:, t, :]).then_inc(mv1_done, 1)
                dve.wait_ge(mv1_done, T // 2 * (half + 1))
                nc.vector.tensor_scalar(ve1[:, tiles], mv1[:, tiles, 1], EPS, None, ALU.add).then_inc(ve1_done, 1)

            def mean_shift(half):
                tiles = slice(T // 2 * half, T // 2 * (half + 1))
                dve.wait_ge(rstd1_done, half + 1)
                nc.vector.scalar_tensor_tensor(shift1[:, tiles], mv1[:, tiles, 0], -1.0, rstd1[:, tiles],
                                               ALU.mult, ALU.mult).then_inc(shift1_done, 1)

            remainder(2, 0)
            h_stats(0)
            with dve.Fori(1, T // 4) as u:
                remainder(2 * u + 1, 1)
                h_stats(2 * u - 1)
                remainder(2 * u + 2, 0)
                h_stats(2 * u)
            remainder(T // 2 + 1, 1)
            h_stats(T // 2 - 1)
            remainder(T // 2 + 2, 0)
            variance1(0)
            for t in range(T // 2 + 3, T - 2):
                remainder(t, t % 2)
                h_stats(t - 3)
            mean_shift(0)
            for t in range(T - 2, T):
                remainder(t, t % 2)
                h_stats(t - 3)
            h_stats(T - 3)
            h_stats(T - 2)

            def place_crossed(t, par):
                dve.wait_ge(xh_set, t + 1)
                for b in range(2):
                    e = 1 - b
                    last = nc.vector.tensor_copy(
                        xblk[par][TOK * e:TOK * e + TOK, b, :].rearrange("p (g e d) -> p g e d", e=2, d=HD)[:, :, e, :],
                        xh[par][TOK * b:TOK * b + TOK, :].rearrange("p (g e d) -> p g e d", e=2, d=HD)[:, :, e, :])
                last.then_inc(xblk_crossed, 1)

            def maximum(t, j):
                dve.wait_ge(scores_done, QUADS * t + j + 1)
                nc.vector.tensor_reduce(rowmax[:, j, :], bank[j][:, 0:D].rearrange("p (h k) -> p h k", k=TOK),
                                        AX_X, ALU.max).then_inc(max_done, 1)

            def shift(t, j):
                dve.wait_ge(max_done, QUADS * t + j + 1)
                nc.vector.tensor_tensor(probs[:, j, :].rearrange("p (h k) -> p h k", k=TOK),
                                        bank[j][:, 0:D].rearrange("p (h k) -> p h k", k=TOK),
                                        rowmax[:, j, :].unsqueeze(2).to_broadcast([P, 4, TOK]),
                                        ALU.subtract).then_inc(shifted, 1)

            def divide(t):
                dve.wait_ge(side_copied, t + 1)
                dve.wait_ge(pv_done, t + 1)
                nc.vector.tensor_tensor(onT[:].rearrange("p a t -> p (a t)"), bank[PV_BANK][:, 0:D],
                                        sideT[:, D:2 * D], ALU.mult).then_inc(on_set, 1)

            def finish(t, par):
                dve.wait_ge(h2b_done, t + 1)
                if not first(t, 2):
                    dve.wait_ge(y_stored[par], 16 * (t // 2) if isinstance(t, int) else (t - par) * 8)
                dve.wait_ge(freq_done, t + 1)
                nc.vector.tensor_tensor(y[par][:], bank[SIDE_BANK][:, 0:D], h2b[par][:], ALU.add).then_inc(y_set, 1)

            def residual(t):
                if not first(t, 1):
                    dve.wait_ge(h2b_done, t)
                dve.wait_ge(proj_done, t + 1)
                nc.vector.tensor_tensor(h2[:], bank[PROJ_BANK][:, 0:D], tile_of(hb_all, t), ALU.add).then_inc(h2_done, 1)
                dve.wait_ge(h2_done, t + 1)
                nc.vector.bn_stats(stats2[:], h2[:]).then_inc(stats2_done, 1)
                dve.wait_ge(stats2_done, t + 1)

            def variance(t):
                nc.vector.bn_aggr(mv2[:], stats2[:]).then_inc(mv2_done, 1)
                dve.wait_ge(mv2_done, t + 1)
                nc.vector.tensor_scalar(ve2[:], mv2[:, 1:2], EPS, None, ALU.add).then_inc(ve2_done, 1)

            def inverse_sums(t):
                dve.wait_ge(half_sums_done, 2 * t + 2)
                nc.vector.tensor_reduce(sums[:].rearrange("p q a e -> p (q a e)"),
                                        half_sums[:].rearrange("p q h k -> p (q h) k"), AX_X,
                                        ALU.add).then_inc(sums_done, 1)
                dve.wait_ge(sums_done, t + 1)
                nc.vector.reciprocal(inv_sum[:], sums[:]).then_inc(inv_done, 1)

            def norm2(t):
                dve.wait_ge(rstd2_done, t + 1)
                nc.vector.tensor_scalar(xh2[:], h2[:], mv2[:, 0:1], rstd2[:, 0:1],
                                        ALU.subtract, ALU.mult).then_inc(xh2_set, 1)

            def step(i, par):
                if has(i - 1) and not at(i, T - 1):
                    finish(i - 1, 1 - par)
                if has(i):
                    residual(i)
                if has(i + 2) and not at(i, -2):
                    place_crossed(i + 2, par)
                if has(i):
                    variance(i)
                if at(i, T - 1):
                    finish(i - 1, 1 - par)
                if has(i + 1):
                    inverse_sums(i + 1)
                if has(i):
                    norm2(i)
                if has(i + 2):
                    maximum(i + 2, 0)
                if has(i + 2):
                    maximum(i + 2, 1)
                    shift(i + 2, 0)
                    maximum(i + 2, 2)
                    shift(i + 2, 1)
                    maximum(i + 2, 3)
                if has(i + 1) and not at(i, -1):
                    divide(i + 1)
                if has(i + 2):
                    shift(i + 2, 2)
                    shift(i + 2, 3)
                if at(i, -1):
                    divide(0)
                if at(i, -2):
                    place_crossed(i + 2, par)

            dve.wait_ge(const_set, 7)
            step(-2, 0)
            h_stats(T - 1)
            variance1(1)
            step(-1, 1)
            dve.wait_ge(hb_done, T // GROUP - 1)
            step(0, 0)
            mean_shift(1)
            step(1, 1)
            dve.wait_ge(hb_done, T // GROUP)
            with dve.Fori(1, T // 2 - 1) as u:
                step(2 * u, 0)
                step(2 * u + 1, 1)
            for i in range(T - 2, T + 1):
                step(i, i % 2)

        @block.tensor
        def _(pe):
            def turn_stacks(t0, n, to):
                for t in range(t0, t0 + n):
                    last = pe.transpose(bank16[to][:, (t - t0) * P:(t - t0 + 1) * P], x_terms[:, t, :], ident16[:])
                last.then_inc(x_turned, 1)

            def turn_wo(chunks):
                for c in chunks:
                    for k in range(HALF):
                        last = pe.transpose(bank[WO_BANK[c]][:, k * P:(k + 1) * P], wo_raw[:, k, bass.ds(c, P, step=NC)],
                                            ident[:])
                    last.then_inc(wo_turned, 1)

            pe.wait_ge(ident_loaded, 16)
            pe.wait_ge(const_set, 5)
            pe.wait_ge(ident16_set, 1)
            pe.wait_ge(w_placed, 3)
            for c in range(NC):
                last = pe.transpose(bank16[0][:, c * P:(c + 1) * P], w_terms[:, c, :], ident16[:])
            last.then_inc(w_turned, 1)
            pe.wait_ge(x_placed, 3)
            turn_stacks(0, 4, 6)
            turn_stacks(4, 4, 7)
            for c in range(HALF):
                last = pe.transpose(bank16[1][:, c * P:(c + 1) * P], w_terms[:, NC + c, :], ident16[:])
            last.then_inc(w_turned, 1)

            def hidden(t, par):
                if not first(t, 2):
                    pe.wait_ge(silu_done, t - 1)
                for c in range(NC):
                    last = pe.matmul(bank[HID_BANK[par]][:, c * P:(c + 1) * P], w_termsT[:, c * P:(c + 1) * P],
                                     x_termsT[:, bass.ds(t * P, P)], start=True, stop=True)
                last.then_inc(hid_done, 1)

            def mix(t, par):
                pe.wait_ge(hi_done, t + 1)
                if not first(t, 2):
                    pe.wait_ge(h_copied, t - 1)
                for w in (wo_hi, wo_lo):
                    if at(t, 0):
                        pe.wait_ge(wo_copied if w is wo_hi else wo_split, NC)
                    for c in range(NC):
                        pe.matmul(bank[MIX_BANK[par]][:, 0:D], hid_hi[:, par, c * P:(c + 1) * P], w[:, c, :],
                                  start=(c == 0 and w is wo_hi), stop=False)
                pe.wait_ge(lo_done, t + 1)
                for c in range(NC):
                    pe.matmul(bank[MIX_BANK[par]][:, 0:D], hid_lo[:, par, c * P:(c + 1) * P], wo_hi[:, c, :],
                              start=False, stop=False)
                pe.matmul(bank[MIX_BANK[par]][:, 0:D], x_termsT[:, bass.ds(t * P, P)], wr_termsT[:],
                          start=False, stop=True).then_inc(mix_done, 1)

            pe.wait_ge(wo_loaded, 16)
            turn_wo((0, 1))
            pe.wait_ge(w_copied, 1)
            pe.wait_ge(x_copied, 1)
            hidden(0, 0)
            turn_wo((2, 3))
            pe.wait_ge(w_copied, 2)
            hidden(1, 1)
            pe.wait_ge(x_copied, 2)
            turn_stacks(8, 8, 7)
            mix(0, 0)
            hidden(2, 0)
            pe.wait_ge(reps_set, 2)
            pe.matmul(bank[4][:, 0:P], wrep[:, 0, :], wrep[:, 1, :], start=True, stop=True).then_inc(small_done, 1)
            pe.matmul(bank[4][:, P:2 * P], erep[:], wrep[:, 2, :], start=True, stop=True).then_inc(small_done, 1)
            pe.wait_ge(wout_loaded, 16)
            for c in range(HALF):
                for k in range(HALF):
                    last = pe.transpose(bank[2 + c][:, k * P:(k + 1) * P], wout_raw[:, k, c * P:(c + 1) * P], ident[:])
                last.then_inc(wout_turned, 1)
            mix(1, 1)
            pe.wait_ge(wout_copied, HALF)
            pe.wait_ge(x_late_copied, 1)
            with pe.Fori(1, T // 2 - 1) as u:
                hidden(2 * u + 1, 1)
                mix(2 * u, 0)
                hidden(2 * u + 2, 0)
                mix(2 * u + 1, 1)

            def scores(t):
                for pair in ((0, 1), (2, 3)):
                    for half in range(HALF):
                        for j in pair:
                            if half == 0 and not first(t, 1):
                                pe.wait_ge(shifted, QUADS * (t - 1) + j + 1)
                            if half == 0 and at(t, 1) and j in (2, 3):
                                pe.wait_ge(value_copied, j - 1)
                            rows32 = slice(32 * j, 32 * j + 32)
                            for b in range(2):
                                last = pe.matmul(bank[j][TOK * b:TOK * b + TOK, half * P:(half + 1) * P],
                                                 qT[rows32, half, TOK * b:TOK * b + TOK],
                                                 xzT[rows32, 2 * half + b, :, :].rearrange("p e k -> p (e k)"),
                                                 start=True, stop=True)
                            if half == HALF - 1:
                                last.then_inc(scores_done, 1)

            def side(i):
                if has(i):
                    pe.wait_ge(p_copied, 2 * i + 1)
                if has(i - 1):
                    pe.wait_ge(xh2_set, i)
                    for half in range(HALF):
                        last = pe.transpose(bank[SIDE_BANK][:, half * P:(half + 1) * P],
                                            xh2[:, half * P:(half + 1) * P], ident[:])
                if has(i):
                    pe.wait_ge(inv_spread, i + 1)
                    for half in range(HALF):
                        last = pe.transpose(bank[SIDE_BANK][:, D + half * P:D + (half + 1) * P],
                                            inv_rows[:, half, :, :].rearrange("p h d -> p (h d)"),
                                            ident[:])
                last.then_inc(side_turned, 1)

            def weigh(t, par):
                pe.wait_ge(xblk_same, t + 1)
                pe.wait_ge(xblk_crossed, t + 1)
                pe.wait_ge(p_copied, 2 * (t + 1))
                for half in range(HALF):
                    for b in range(2):
                        for j in range(QUADS):
                            last = pe.matmul(bank[PV_BANK][32 * j:32 * j + 32, half * P + TOK * b:half * P + TOK * (b + 1)],
                                             xblk[par][:, b, half * P + 32 * j:half * P + 32 * j + 32],
                                             pT[:, 2 * j + half, TOK * b:TOK * b + TOK], start=True, stop=True)
                last.then_inc(pv_done, 1)

            def mix_freq(t):
                pe.wait_ge(side_copied, t + 2)
                if at(t, 0):
                    pe.wait_ge(mixw_copied, HALF)
                for half in range(HALF):
                    last = pe.matmul(bank[SIDE_BANK][:, 0:D], sideT[:, half * P:(half + 1) * P], mix_w[:, half, :],
                                     start=(half == 0), stop=(half == HALF - 1))
                last.then_inc(freq_done, 1)

            def project(t):
                pe.wait_ge(on_set, t + 1)
                if isinstance(t, int) and t < HALF:
                    pe.wait_ge(mixw_copied, t + 1)
                if not first(t, 1):
                    pe.wait_ge(h2_done, t)
                for half in range(HALF):
                    last = pe.matmul(bank[PROJ_BANK][:, 0:D], onT[:, half, :], value_w[:, half, :],
                                     start=(half == 0), stop=(half == HALF - 1))
                last.then_inc(proj_done, 1)

            def turn_x(t, par):
                pe.wait_ge(xh_set, t + 1)
                if not first(t, 2):
                    pe.wait_ge(p_copied, 2 * (t - 1))
                for half in range(HALF):
                    last = pe.transpose(bank[T1_BANK][:, half * P:(half + 1) * P], xh[par][:, half * P:(half + 1) * P],
                                        ident[:])
                last.then_inc(x1_turned, 1)

            def turn_p(t, part):
                pe.wait_ge(exp_done, QUADS * t + 2 * part + 2)
                if part == 0 and not first(t, 2):
                    pe.wait_ge(y_set, t - 1)
                if part == 1 and has(t + 1):
                    pe.wait_ge(xzT_copied, 2 * (t + 2))
                for k in range(4):
                    j, half = 2 * part + k // 2, k % 2
                    last = pe.transpose(bank[(SIDE_BANK, T1_BANK)[part]][:, k * P:(k + 1) * P],
                                        probs[:, j, half * P:(half + 1) * P], ident[:])
                last.then_inc(p_turned, 1)

            def query(t):
                pe.wait_ge(xT_copied, t + 1)
                if not first(t, 2):
                    pe.wait_ge(on_set, t - 1)
                for half in range(HALF):
                    last = pe.matmul(bank[PV_BANK][:, half * P:(half + 1) * P], score_w[:],
                                     xT[:, half * P:(half + 1) * P], start=True, stop=True)
                last.then_inc(q_done, 1)

            def value_weights():
                pe.wait_ge(shifted, QUADS)
                for c in range(HALF):
                    pe.matmul(bank[2 + c][:, 0:D], wv_blocks[:], woutT[:, c, :], start=True, stop=True).then_inc(value_done, 1)

            def rows_spectrum(c):
                pe.wait_ge(cols_set, 4)
                pe.matmul(bank[HALFWAY_BANK[c]][:, 0:D], cols[:, 2 * c, :], cosine[:], start=True, stop=False)
                pe.matmul(bank[HALFWAY_BANK[c]][:, 0:D], cols[:, 2 * c + 1, :], sine[:], start=False,
                          stop=True).then_inc(halfway_done, 1)

            def cols_spectrum(c):
                pe.wait_ge(halfway_copied, 2)
                if c == 1:
                    pe.wait_ge(h2_done, 1)
                pe.matmul(bank[PROJ_BANK][:, 0:D], halfway[:, 0, c * P:(c + 1) * P], cosine[:], start=True, stop=False)
                pe.matmul(bank[PROJ_BANK][:, 0:D], halfway[:, 1, c * P:(c + 1) * P], sine[:], start=False,
                          stop=True).then_inc(mixw_done, 1)

            def step(i, par):
                if has(i + 1):
                    pe.wait_ge(xzT_copied, 2 * (i + 2))
                    pe.wait_ge(q_copied, i + 2)
                    scores(i + 1)
                if at(i, 1):
                    cols_spectrum(1)
                side(i)
                if has(i):
                    weigh(i, par)
                if has(i + 2):
                    turn_x(i + 2, par)
                if at(i, T - 1):
                    project(i)
                mix_freq(i - 1)
                if has(i) and not at(i, T - 1):
                    project(i)
                if has(i + 2):
                    query(i + 2)
                if has(i + 1):
                    turn_p(i + 1, 0)
                    turn_p(i + 1, 1)

            hidden(T - 1, 1)
            rows_spectrum(0)
            turn_x(0, 0)
            mix(T - 2, 0)
            query(0)
            mix(T - 1, 1)
            pe.wait_ge(silu_done, T)
            pe.wait_ge(halfway_copied, 1)
            pe.wait_ge(xzT_copied, 2)
            pe.wait_ge(q_copied, 1)
            scores(0)
            turn_x(1, 1)
            pe.wait_ge(h_copied, T)
            rows_spectrum(1)
            query(1)
            turn_p(0, 0)
            value_weights()
            turn_p(0, 1)
            pe.wait_ge(xzT_copied, 4)
            pe.wait_ge(q_copied, 2)
            scores(1)
            cols_spectrum(0)
            side(0)
            weigh(0, 0)
            turn_x(2, 0)
            pe.wait_ge(side_copied, 1)
            turn_p(1, 0)
            project(0)
            query(2)
            turn_p(1, 1)
            step(1, 1)
            with pe.Fori(1, T // 2 - 1) as u:
                step(2 * u, 0)
                step(2 * u + 1, 1)
            for i in range(T - 2, T + 1):
                step(i, i % 2)


_INS = {
    "x": "x", "L0_tok_W_h": "W_h", "L0_tok_b_h": "b_h", "L0_tok_W_o": "W_o", "L0_tok_b_o": "b_o",
    "L0_tok_W_r": "W_r", "L0_tok_b_r": "b_r", "L0_attn_Wq": "Wq", "L0_attn_Wk": "Wk", "L0_attn_Wv": "Wv",
    "L0_attn_W_out": "W_out", "L0_attn_b_out": "b_out", "L0_ffn_w_freq_real": "wr", "L0_ffn_w_freq_imag": "wi",
    "L0_ffn_bias": "bias",
}


def kernel(**inputs):
    import concourse.bacc as _bacc
    from concourse.bass_utils import run_bass_kernel_spmd as _run

    nc = _bacc.Bacc("TRN2", target_bir_lowering=False, num_devices=1)
    arrays, args = {}, {}
    data = {short: np.asarray(inputs[name]) for name, short in _INS.items()}
    for short in ("wr", "wi"):
        data[short] = data[short][FOLDED][:, FOLDED]
    data.update(launch_constants())
    for short, v in data.items():
        v = np.ascontiguousarray(v)
        arrays[f"in_{short}"] = v
        args[short] = nc.dram_tensor(f"in_{short}", v.shape, mybir.dt.from_np(v.dtype), kind="ExternalInput").ap()
    out = nc.dram_tensor("out_0", (BATCH, TOK, D), F32, kind="ExternalOutput").ap()
    audio_tower_kernel(nc, args, out)
    r = _run(nc, [arrays], core_ids=[0])
    return r.results[0]["out_0"]
```
